# Optimizing a Trainium2 kernel written in Bass

```python
import numpy as np
import jax
import jax.numpy as jnp

def _softmax(x, axis=-1):
    return jax.nn.softmax(x, axis=axis)

def _gelu(x):
    return jax.nn.gelu(x, approximate=True)

def _silu(x):
    return jax.nn.silu(x)

def _sigmoid(x):
    return jax.nn.sigmoid(x)

def _layernorm(x, axis=-1, eps=1e-05):
    m = jnp.mean(x, axis=axis, keepdims=True)
    v = jnp.var(x, axis=axis, keepdims=True)
    return (x - m) / jnp.sqrt(v + eps)

def _scatter_add(tgt, idx, src, axis=0):
    return tgt.at[idx].add(src)

def _segment_sum(src, seg, n):
    return jax.ops.segment_sum(src, seg, n)
kernel_name = 'mk_decoder_preln_d1_seqx_r4_ef3fed'

def setup_inputs(seed: int=0):
    np.random.seed(seed)
    _w = jnp.asarray

    def _rec_inputs():
        import jax
        import jax.numpy as jnp
        _rk = jax.random.key(seed)
        x = 7.22e-05 + 1 * jax.random.normal(jax.random.fold_in(_rk, 1), (64, 128, 256), jnp.float32)
        _lenS = 128 - jax.random.randint(jax.random.fold_in(_rk, 7), (64,), 0, max(1, 128 // 4) + 1, jnp.int32)
        _lenS2 = 128 - jax.random.randint(jax.random.fold_in(_rk, 8), (64,), 0, max(1, 128 // 4) + 1, jnp.int32)
        _ctx_1024P = jax.random.normal(jax.random.fold_in(_rk, 11), (64, 16, 256), jnp.float32)
        _ctx_1024c = jax.random.dirichlet(jax.random.fold_in(_rk, 511), 0.3 * jnp.ones((16,), jnp.float32), (64, 128))
        _ctx_1024t = jnp.einsum('bsk,bkd->bsd', _ctx_1024c, _ctx_1024P)
        _ctx_1024t = _ctx_1024t * jax.lax.rsqrt(jnp.mean(jnp.square(_ctx_1024t)) + 1e-12) * 0.953939
        ctx_1024 = 4.13588e-05 + 0.999923 * (_ctx_1024t + 0.3 * jax.random.normal(jax.random.fold_in(_rk, 611), (64, 128, 256), jnp.float32))
        return (x, ctx_1024)
    x, ctx_1024 = _rec_inputs()

    def _L0_attn_setup():
        import math
        import jax, jax.numpy as jnp
        import numpy as np
        B, L, D, H = (4, 1024, 256, 16)
        D_K = D // H
        FACTOR = 5
        U = min(max(1, int(FACTOR * math.log(L + 1))), L)
        key = jax.random.key(seed)
        ks = jax.random.split(key, 10)
        s = 1.0 / math.sqrt(D)
        return {'x': jax.random.normal(ks[0], (B, L, D), jnp.float32), 'W_q': jax.random.normal(ks[1], (D, D), jnp.float32) * s, 'b_q': jax.random.normal(ks[2], (D,), jnp.float32) * s, 'W_k': jax.random.normal(ks[3], (D, D), jnp.float32) * s, 'b_k': jax.random.normal(ks[4], (D,), jnp.float32) * s, 'W_v': jax.random.normal(ks[5], (D, D), jnp.float32) * s, 'b_v': jax.random.normal(ks[6], (D,), jnp.float32) * s, 'W_o': jax.random.normal(ks[7], (D, D), jnp.float32) * s, 'b_o': jax.random.normal(ks[8], (D,), jnp.float32) * s, 'k_sample_idx': jax.random.randint(ks[9], (U,), 0, L, jnp.int32)}
    _L0_attn_all = _L0_attn_setup()
    _L0_attn_in = {k: v for k, v in _L0_attn_all.items() if k in ('W_q', 'b_q', 'W_k', 'b_k', 'W_v', 'b_v', 'W_o', 'b_o', 'k_sample_idx')}
    del _L0_attn_all

    def _L0_xattn_setup():
        import jax, jax.numpy as jnp
        import numpy as np
        BETA = 256
        NUM_HEADS = 16
        NORM = (BETA // NUM_HEADS) ** (-0.5)
        key = jax.random.key(seed)
        ks = jax.random.split(key, 6)
        B, N = (4, 512)
        D_in_q = D_in_k = D_in_v = 256
        D_out_k = D_out_v = 256
        q = jax.random.normal(ks[0], (B, N, D_in_q), dtype=jnp.float32)
        k = jax.random.normal(ks[1], (B, N, D_in_k), dtype=jnp.float32)
        v = jax.random.normal(ks[2], (B, N, D_in_v), dtype=jnp.float32)
        Wq = jax.random.normal(ks[3], (D_out_k, D_in_q), dtype=jnp.float32) * D_in_q ** (-0.5)
        Wk = jax.random.normal(ks[4], (D_out_k, D_in_k), dtype=jnp.float32) * D_in_k ** (-0.5)
        Wv = jax.random.normal(ks[5], (D_out_v, D_in_v), dtype=jnp.float32) * D_in_v ** (-0.5)
        return {'q': q, 'k': k, 'v': v, 'Wq': Wq, 'Wk': Wk, 'Wv': Wv}
    _L0_xattn_all = _L0_xattn_setup()
    _L0_xattn_in = {k: v for k, v in _L0_xattn_all.items() if k in ('Wq', 'Wk', 'Wv')}
    del _L0_xattn_all

    def _L0_ffn_setup():
        import jax, jax.numpy as jnp
        import numpy as np
        B, S, D, O, E, K = (2, 512, 256, 256, 8, 2)
        key = jax.random.key(seed)
        ks = jax.random.split(key, 6)

        def w(k, shape, fan_in):
            return jax.random.normal(k, shape, jnp.float32) * fan_in ** (-0.5)
        return {'x': jax.random.normal(ks[0], (B, S, D), jnp.float32), 'gate_w': w(ks[1], (E, D), D), 'gate_b': jnp.zeros((E,), jnp.float32), 'w1': w(ks[2], (E, D, O), D), 'b1': jnp.zeros((E, O), jnp.float32), 'w2': w(ks[3], (E, O, O), O), 'b2': jnp.zeros((E, O), jnp.float32), 'w3': w(ks[4], (E, O, O), O), 'b3': jnp.zeros((E, O), jnp.float32)}
    _L0_ffn_all = _L0_ffn_setup()
    _L0_ffn_in = {k: v for k, v in _L0_ffn_all.items() if k in ('gate_w', 'gate_b', 'w1', 'b1', 'w2', 'b2', 'w3', 'b3')}
    del _L0_ffn_all
    return {'x': x, 'ctx_1024': ctx_1024, 'L0_attn_W_q': _L0_attn_in['W_q'], 'L0_attn_b_q': _L0_attn_in['b_q'], 'L0_attn_W_k': _L0_attn_in['W_k'], 'L0_attn_b_k': _L0_attn_in['b_k'], 'L0_attn_W_v': _L0_attn_in['W_v'], 'L0_attn_b_v': _L0_attn_in['b_v'], 'L0_attn_W_o': _L0_attn_in['W_o'], 'L0_attn_b_o': _L0_attn_in['b_o'], 'L0_attn_k_sample_idx': _L0_attn_in['k_sample_idx'], 'L0_xattn_Wq': _L0_xattn_in['Wq'], 'L0_xattn_Wk': _L0_xattn_in['Wk'], 'L0_xattn_Wv': _L0_xattn_in['Wv'], 'L0_ffn_gate_w': _L0_ffn_in['gate_w'], 'L0_ffn_gate_b': _L0_ffn_in['gate_b'], 'L0_ffn_w1': _L0_ffn_in['w1'], 'L0_ffn_b1': _L0_ffn_in['b1'], 'L0_ffn_w2': _L0_ffn_in['w2'], 'L0_ffn_b2': _L0_ffn_in['b2'], 'L0_ffn_w3': _L0_ffn_in['w3'], 'L0_ffn_b3': _L0_ffn_in['b3']}

def reference(x, ctx_1024, L0_attn_W_q, L0_attn_b_q, L0_attn_W_k, L0_attn_b_k, L0_attn_W_v, L0_attn_b_v, L0_attn_W_o, L0_attn_b_o, L0_attn_k_sample_idx, L0_xattn_Wq, L0_xattn_Wk, L0_xattn_Wv, L0_ffn_gate_w, L0_ffn_gate_b, L0_ffn_w1, L0_ffn_b1, L0_ffn_w2, L0_ffn_b2, L0_ffn_w3, L0_ffn_b3):
    import jax
    import jax.numpy as jnp

    def _L0_attn_ref(x, W_q, b_q, W_k, b_k, W_v, b_v, W_o, b_o, k_sample_idx):
        import math
        import jax, jax.numpy as jnp
        import numpy as np
        B, L, D, H = (4, 1024, 256, 16)
        D_K = D // H
        FACTOR = 5
        U = min(max(1, int(FACTOR * math.log(L + 1))), L)
        b, l, d = x.shape
        Q = (x @ W_q + b_q).reshape(b, l, H, D_K).transpose(0, 2, 1, 3)
        K = (x @ W_k + b_k).reshape(b, l, H, D_K).transpose(0, 2, 1, 3)
        V = (x @ W_v + b_v).reshape(b, l, H, D_K).transpose(0, 2, 1, 3)
        K_sample = K[:, :, k_sample_idx, :]
        QKs = jnp.einsum('bhld,bhud->bhlu', Q, K_sample)
        M = QKs.max(axis=-1) - QKs.mean(axis=-1)
        u = k_sample_idx.shape[0]
        _, top_idx = jax.lax.top_k(M, u)
        Q_sparse = jnp.take_along_axis(Q, top_idx[..., None], axis=2)
        scale = math.sqrt(D_K)
        attn = jax.nn.softmax(jnp.einsum('bhud,bhld->bhul', Q_sparse, K) / scale, axis=-1)
        sparse_out = jnp.einsum('bhul,bhld->bhud', attn, V)
        context = jnp.broadcast_to(V.mean(axis=2, keepdims=True), V.shape)
        b_idx = jnp.arange(b)[:, None, None]
        h_idx = jnp.arange(H)[None, :, None]
        context = context.at[b_idx, h_idx, top_idx].set(sparse_out)
        context = context.transpose(0, 2, 1, 3).reshape(b, l, d)
        return context @ W_o + b_o

    def _L0_xattn_ref(q, k, v, Wq, Wk, Wv):
        import jax, jax.numpy as jnp
        import numpy as np
        BETA = 256
        NUM_HEADS = 16
        NORM = (BETA // NUM_HEADS) ** (-0.5)
        qp = jax.nn.relu(jnp.einsum('bnd,od->bno', q, Wq))
        kp = jax.nn.relu(jnp.einsum('bnd,od->bno', k, Wk))
        vp = jax.nn.relu(jnp.einsum('bnd,od->bno', v, Wv))
        B, N, D = qp.shape
        dh = D // NUM_HEADS
        qh = qp.reshape(B, N, NUM_HEADS, dh)
        kh = kp.reshape(B, N, NUM_HEADS, dh)
        vh = vp.reshape(B, N, NUM_HEADS, vp.shape[-1] // NUM_HEADS)
        E = NORM * jnp.einsum('bqhd,bkhd->bhqk', qh, kh)
        A = jax.nn.softmax(E, axis=-1)
        out = jnp.einsum('bhqk,bkhd->bqhd', A, vh)
        return out.reshape(B, N, -1)

    def _L0_ffn_ref(x, gate_w, gate_b, w1, b1, w2, b2, w3, b3):
        import jax, jax.numpy as jnp
        import numpy as np
        B, S, D, O, E, K = (2, 512, 256, 256, 8, 2)
        probs = jax.nn.softmax(x @ gate_w.T + gate_b, axis=-1)
        _, topi = jax.lax.top_k(probs, K)
        onehot = jax.nn.one_hot(topi, E, dtype=probs.dtype)
        cw = jnp.einsum('bske,bsk->bse', onehot, probs[..., :K])
        out = jnp.zeros(x.shape[:2] + (O,), x.dtype)
        for e in range(E):
            h = jax.nn.relu(x @ w1[e] + b1[e])
            h = jax.nn.relu(h @ w2[e] + b2[e])
            h = h @ w3[e] + b3[e]
            out = out + cw[..., e:e + 1] * h
        return out
    x = x + _L0_attn_ref(_layernorm(x, axis=-1), L0_attn_W_q, L0_attn_b_q, L0_attn_W_k, L0_attn_b_k, L0_attn_W_v, L0_attn_b_v, L0_attn_W_o, L0_attn_b_o, L0_attn_k_sample_idx)
    x = x + _L0_xattn_ref(_layernorm(x, axis=-1), ctx_1024, ctx_1024, L0_xattn_Wq, L0_xattn_Wk, L0_xattn_Wv)
    x = x + _L0_ffn_ref(_layernorm(x, axis=-1), L0_ffn_gate_w, L0_ffn_gate_b, L0_ffn_w1, L0_ffn_b1, L0_ffn_w2, L0_ffn_b2, L0_ffn_w3, L0_ffn_b3)
    return x

_drawn_inputs = setup_inputs


def setup_inputs(seed=0):
    import zlib

    import numpy as np

    out = dict(_drawn_inputs(seed))
    spreads = {'L0_ffn_gate_b': (0.0, 0.1),
     'L0_ffn_b1': (0.0, 0.794),
     'L0_ffn_b2': (0.0, 0.561),
     'L0_ffn_b3': (0.0, 0.386)}
    factors = {'L0_attn_b_q': 3.312, 'L0_attn_b_k': 8.0}
    for name, (base, spread) in spreads.items():
        noise = np.random.default_rng([zlib.crc32(name.encode()), seed]).standard_normal(out[name].shape)
        drawn = base * np.exp(spread * noise) if base else spread * noise
        out[name] = jnp.asarray(drawn.astype(out[name].dtype))
    for name, factor in factors.items():
        out[name] = (out[name] * factor).astype(out[name].dtype)
    return out
```

```python
import concourse.bass as bass
from concourse import mybir
from contextlib import ExitStack

B, L, D, H, U, NE = 64, 128, 256, 16, 34, 8
DH = D // H
NC = D // 128
HQ = 4
NQ = H // HQ
UM = U + 1
HS = 32
GT = 4
NG = B // GT
EPS = 1e-5
GONE = -3.0e38


def decoder_block(nc, x, ctx, wq, bq, wk, bk, wv, bv, wo, bo, sidx, xwqT, xwkT, xwvT,
                  gwT, gb, w1, b1, w2, b2, w3, b3, ident_d, hmask_d, iota8_d, kcol_d, out):
    f32, i32, u32 = mybir.dt.float32, mybir.dt.int32, mybir.dt.uint32
    ALU, ACT, AX = mybir.AluOpType, mybir.ActivationFunctionType, mybir.AxisListType.X

    st = ExitStack()
    with st:
        def sb(name, shape, dt=f32):
            return st.enter_context(nc.sbuf_tensor(name, shape, dt))

        def sem(name):
            return st.enter_context(nc.semaphore(name))

        bank = [st.enter_context(nc.psum_tensor(f"bank{i}", [128, 512], f32)) for i in range(8)]
        ps_s = {"b": bank[0], "d": bank[1]}
        ps_at = bank[2]
        ps_o = {"b": bank[3], "d": bank[4]}
        m0, m1, m2 = bank[5], bank[6], bank[7]

        ident = sb("ident", [128, 128])
        hmask = sb("hmask", [128, HQ])
        iota8 = sb("iota8", [128, NE])
        kcol = sb("kcol", [128, 1])
        mean_w = sb("mean_w", [128, 128])
        epsc = sb("epsc", [128, GT])
        mhalf = sb("mhalf", [128, GT])
        wq_s, wo_s = sb("wq_s", [128, NC, D]), sb("wo_s", [128, NC, D])
        wkv_s = sb("wkv_s", [128, NC, 2 * D])
        xwq_s, xwk_s, xwv_s = (sb(n, [128, NC, D]) for n in ("xwq_s", "xwk_s", "xwv_s"))
        bq_s = sb("bq_s", [128, NC])
        bk_s, bv_s, bo_s = (sb(n, [128, D]) for n in ("bk_s", "bv_s", "bo_s"))
        idx_i, idx_f, idx_n = sb("idx_i", [128, U], i32), sb("idx_f", [128, U]), sb("idx_n", [128, U])
        samp = sb("samp", [128, UM])
        w_s = [sb(f"w{n + 1}_s", [128, NE, NC, D]) for n in range(3)]
        b1_s, b2_s = sb("b1_s", [128, NE, NC]), sb("b2_s", [128, NE, NC])
        b3_s = sb("b3_s", [NE, D])
        gw_s, gb_s = sb("gw_s", [128, NC, NE]), sb("gb_s", [128, NE])

        xall = sb("xall", [128, B, D])

        xn = sb("xn", [128, 2, D])
        xnT = sb("xnT", [128, NC, L])
        ktok = sb("ktok", [128, D])
        kT = sb("kT", [128, NC, L])
        qT = {"b": sb("qT", [128, 2, NC, L]), "d": sb("xqT", [128, 2, NC, L])}
        kbd = {"b": sb("kbd", [128, 2, NC, HQ, L]), "d": sb("xkbd", [128, 2, NC, HQ, L])}
        vh = {"b": sb("vh", [128, 2, H, HS]), "d": sb("xvh", [128, 2, H, HS])}
        mean_v = sb("mean_v", [128, 2, D])
        ksbd = sb("ksbd", [128, NC, HQ, UM])
        smax = sb("smax", [128, H])
        mtok = sb("mtok", [128, 2, H])
        mT = [sb("mT0", [32, L]), sb("mT1", [32, L])]
        top8 = sb("top8", [32, 8])
        top2 = sb("top2", [32, 8])
        selT = sb("selT", [32, L])
        sel, nsel = sb("sel", [128, 2, H]), sb("nsel", [128, 2, H])
        mx = {"b": sb("mx", [128, HQ]), "d": sb("xmx", [128, HQ])}
        pr = {"b": sb("pr", [128, HQ, L]), "d": sb("xpr", [128, HQ, L])}
        prT = {"b": sb("prT", [128, HQ, L]), "d": sb("xprT", [128, HQ, L])}
        oT = {"b": sb("oT", [128, NQ, L]), "d": sb("xoT", [128, NQ, L])}
        rden, wsel = sb("rden", [128, H]), sb("wsel", [128, H])
        xrden = sb("xrden", [128, H])
        ctxa, ctxv, umean = sb("ctxa", [128, D]), sb("ctxv", [128, D]), sb("umean", [128, D])
        ctxT = sb("ctxT", [128, NC, L])
        xn2, xn2T = sb("xn2", [128, D]), sb("xn2T", [128, NC, L])
        xatt = sb("xatt", [128, D])
        cin = sb("cin", [128, 2, D])
        cT, xkT = sb("cT", [128, NC, L]), sb("xkT", [128, NC, L])
        stl, agl, rsl = sb("stl", [128, 6]), sb("agl", [128, 2]), sb("rsl", [128, 2])
        stc, agc, rsc = sb("stc", [128, 6]), sb("agc", [128, 2]), sb("rsc", [128, 2])

        st3, ag3, rs3 = sb("st3", [128, GT, 6]), sb("ag3", [128, GT, 2]), sb("rs3", [128, 2, GT])
        xn3 = kbd["d"][:, 0, :, :, :].rearrange("p c j l -> p (c j l)").rearrange("p (t n) -> p t n", t=GT)
        x3T = kbd["d"][:, 1, :, :, :].rearrange("p c j l -> p c (j l)")
        lg, pe_ = sb("lg", [128, GT, NE]), sb("pe_", [128, GT, NE])
        gm, gs = sb("gm", [128, GT]), sb("gs", [128, GT])
        pt8, pi8, pf8 = sb("pt8", [128, GT, 8]), sb("pi8", [128, GT, 8], u32), sb("pf8", [128, GT, 8])
        oh0, cw, cwT = sb("oh0", [128, GT, NE]), sb("cw", [128, GT, NE]), sb("cwT", [NE, GT, L])
        h1, h2 = (kbd["b"][:, n, :, :, :].rearrange("p c j l -> p c (j l)") for n in range(2))

        S = {}

        def s(name):
            if name not in S:
                S[name] = sem(name)
            return S[name]

        block = st.enter_context(nc.Block())

        STEPS = B + 5
        PRO, LAST = 3, B // 2
        BODIES = (STEPS + 1) // 2

        ANY = 1 << 20

        def is_int(v):
            return isinstance(v, int)

        def on(t):
            return not is_int(t) or 0 <= t < B

        def ge(eng, name, v, most=B):
            if is_int(v):
                v = min(v, most)
                if v <= 0:
                    return
            eng.wait_ge(s(name), v)

        def alone(eng):
            eng.sem_inc(s("passed"), 1)

        def run_bodies(eng, step):
            for i in range(PRO):
                for par in range(2):
                    step(2 * i + par, i, par)
            with eng.Fori(PRO, LAST) as i:
                for par in range(2):
                    step(i * 2 + par, i, par)
            for i in range(LAST, BODIES):
                for par in range(2):
                    step(2 * i + par, i, par)

        def quads(u):
            return {-2: ("b", u - 3, 3), -1: ("d", u - 5, 3),
                    **{2 * g: ("b", u - 2, g) for g in range(NQ)},
                    **{2 * g + 1: ("d", u - 4, g) for g in range(NQ)}}

        def parity(par, back):
            return (par + back) % 2

        @block.sync
        def _(sp):
            for dst, src in ((ident[:, :], ident_d), (hmask[:, :], hmask_d), (iota8[:, :], iota8_d),
                             (kcol[:, :], kcol_d)):
                sp.dma_start(dst, src).then_inc(s("const_in"), 16)
            for dst, src in ((wq_s, wq), (wo_s, wo)):
                sp.dma_start(dst[:, :, :], src.rearrange("(c p) n -> p c n", p=128)).then_inc(s("const_in"), 16)
            sp.dma_start(wkv_s[:, :, 0:D], wk.rearrange("(c p) n -> p c n", p=128)).then_inc(s("const_in"), 16)
            sp.dma_start(wkv_s[:, :, D:2 * D], wv.rearrange("(c p) n -> p c n", p=128)).then_inc(s("const_in"), 16)
            for dst, src in ((xwq_s, xwqT), (xwk_s, xwkT), (xwv_s, xwvT)):
                sp.dma_start(dst[:, :, :], src.rearrange("(c p) n -> p c n", p=128)).then_inc(s("const_in"), 16)
            with nc.allow_non_contiguous_dma(reason="small vectors, once"):
                sp.dma_start(bq_s[:, :], bq.rearrange("(c p) -> p c", p=128)).then_inc(s("const_in"), 16)
                for dst, src, n in ((bk_s, bk, D), (bv_s, bv, D), (bo_s, bo, D), (idx_i, sidx, U), (gb_s, gb, NE)):
                    sp.dma_start(dst[:, :], src.rearrange("(a n) -> a n", a=1).to_broadcast([128, n])).then_inc(s("const_in"), 16)

            def step(u, i, par):
                if on(u):
                    ge(sp, f"x_in{par}", i * 16, 16 * B)
                    alone(sp)
                    sp.dma_start(xall[:, bass.ds(u, 1), :], x[bass.ds(u, 1), :, :].rearrange("b p n -> p b n"))\
                        .then_inc(s(f"x_in{par}"), 16)
                t, j = u - 2, i - 1
                if on(t):
                    ge(sp, f"ctx_in{par}", j * 16, 16 * B)
                    alone(sp)
                    ge(sp, "e_transposed", t - 1)
                    alone(sp)
                    sp.dma_start(cin[:, par, :], ctx[bass.ds(t, 1), :, :].rearrange("b p n -> p (b n)"))\
                        .then_inc(s(f"ctx_in{par}"), 16)

            run_bodies(sp, step)

        CONST = 17
        EXPERT_LOADS = 7

        @block.gpsimd
        def _(pool):
            pool.memset(mean_w[:, :], 1.0 / L)
            pool.memset(epsc[:, :], EPS)
            pool.memset(mhalf[:, :], -0.5)
            for k in "bd":
                pool.memset(vh[k][:, :, :, :], 0.0).then_inc(s("zeroed"), 1)
            pool.wait_ge(s("zeroed"), 2)
            for k in "bd":
                pool.memset(vh[k][:, :, :, DH:DH + 1], 1.0).then_inc(s("ones_set"), 1)
            pool.wait_ge(s("ones_set"), 2)
            pool.memset(top2[:, :], GONE).then_inc(s("pool_const"), 1)

            def rstd(aggr, rs, name, t):
                ge(pool, f"{name}_aggr", t + 1)
                pool.tensor_tensor(rs[:, 0:1], aggr[:, 1:2], epsc[:, 0:1], ALU.add).then_inc(s(f"{name}_veps"), 1)
                ge(pool, f"{name}_veps", t + 1)
                pool.tensor_tensor(rs[:, 1:2], rs[:, 0:1], mhalf[:, 0:1], ALU.pow).then_inc(s(f"{name}_rstd"), 1)

            def blocks(k, src, name, t, p):
                ge(pool, f"{name}_kT", t + 1)
                ge(pool, f"{k}_scores", 4 * t - 4, 4 * B)
                pool.tensor_tensor(kbd[k][:, p, :, :, :],
                                   src[:, :, :].unsqueeze(2).to_broadcast([128, NC, HQ, L]),
                                   hmask[:, :].unsqueeze(1).unsqueeze(3).to_broadcast([128, NC, HQ, L]),
                                   ALU.mult).then_inc(s(f"{k}_keys"), 1)

            pool.wait_ge(s("const_in"), 16 * CONST)

            def step(u, i, par):
                t, p = u - 3, parity(par, 3)
                if on(t):
                    ge(pool, "l_xn", t + 1)
                    pool.tensor_tensor(xall[:, bass.ds(t, 1), :].rearrange("p b n -> p (b n)"),
                                       xall[:, bass.ds(t, 1), :].rearrange("p b n -> p (b n)"),
                                       bo_s[:, :], ALU.add).then_inc(s("c_xb"), 1)
                    j = (i - 1) if par else (i - 2)
                    ge(pool, "k_sel", j + 1)
                    ge(pool, "a_mean", t + 1)
                    ge(pool, "c_context", t)
                    pool.tensor_tensor(umean[:, :].rearrange("p (h d) -> p h d", h=H),
                                       mean_v[:, p, :].rearrange("p (h d) -> p h d", h=H),
                                       nsel[:, p, :].unsqueeze(2).to_broadcast([128, H, DH]),
                                       ALU.mult).then_inc(s("c_umean"), 1)
                    rstd(agc, rsc, "c", t)
                if on(u - 1):
                    blocks("b", kT, "a", u - 1, parity(par, 1))
                if on(u):
                    rstd(agl, rsl, "l", u)
                if on(t):
                    blocks("d", xkT, "e", t, p)

            run_bodies(pool, step)

            def group(g):
                ge(pool, "f_aggr", g + 1, ANY)
                pool.tensor_tensor(rs3[:, 0, :], ag3[:, :, 1], epsc[:, :], ALU.add).then_inc(s("f_veps"), 1)
                ge(pool, "f_veps", g + 1, ANY)
                pool.tensor_tensor(rs3[:, 1, :], rs3[:, 0, :], mhalf[:, :], ALU.pow).then_inc(s("f_rstd"), 1)

            group(0)
            with pool.Fori(1, NG) as g:
                group(g)

        @block.scalar
        def _(act):
            for dst, src in zip(w_s, (w1, w2, w3)):
                act.dma_start(dst[:, :, :, :], src.rearrange("e (c p) n -> p e c n", p=128)).then_inc(s("experts_in"), 16)
            with nc.allow_non_contiguous_dma(reason="small vectors, once"):
                for dst, src in ((b1_s, b1), (b2_s, b2)):
                    act.dma_start(dst[:, :, :], src.rearrange("e (c p) -> p e c", p=128)).then_inc(s("experts_in"), 16)
                act.dma_start(b3_s[:, :], b3).then_inc(s("experts_in"), 16)
                act.dma_start(gw_s[:, :, :], gwT.rearrange("(c p) n -> p c n", p=128)).then_inc(s("experts_in"), 16)
            act.wait_ge(s("const_in"), 16 * CONST)
            act.wait_ge(s("pool_const"), 1)

            def exp(k, t, g):
                ge(act, f"{k}_shifted", 4 * t + g + 1, 4 * B)
                act.activation(pr[k][:, :, :], pr[k][:, :, :], ACT.Exp, scale=DH ** -0.5).then_inc(s(f"{k}_probs"), 1)

            def copy_T(k, t, g):
                ge(act, f"{k}_probsT", 4 * t + g + 1, 4 * B)
                ge(act, f"{k}_pv", 4 * t + g, 4 * B)
                act.activation(prT[k][:, :, :], ps_at[:, :].rearrange("p (j l) -> p j l", j=HQ), ACT.Copy)\
                    .then_inc(s(f"{k}_prT"), 1)

            def copy_o(k, t, name):
                ge(act, f"{k}_pv", 4 * t + 4, 4 * B)
                ge(act, f"{name}_oT_turned", t)
                act.activation(oT[k][:, :, :], ps_o[k][:, :].rearrange("p (g l) -> p g l", g=NQ), ACT.Copy)\
                    .then_inc(s(f"{k}_oT"), 1)

            def two(src):
                return src[:, 0:NC * L].rearrange("p (c l) -> p c l", c=NC)

            def step(u, i, par):
                q = quads(u)
                tA, pA, tC, pC, tG = u - 1, parity(par, 1), u - 3, parity(par, 3), u - 5
                for m in range(8):
                    if m == 1 and on(tC):
                        copy_o("b", tC, "c")
                    if m == 1 and on(tA):
                        ge(act, "a_transposed", tA + 1)
                        ge(act, "a_projected", tA)
                        act.activation(xnT[:, :, :], two(m0), ACT.Copy).then_inc(s("a_xnT"), 1)
                    if m == 2 and on(tC):
                        ge(act, "e_transposed", tC + 1)
                        ge(act, "e_projected", tC)
                        act.activation(cT[:, :, :], two(m2), ACT.Copy).then_inc(s("e_cT"), 1)
                    if m == 2 and on(tG):
                        copy_o("d", tG, "g")
                    if m == 3 and on(tA):
                        ge(act, "a_projected", tA + 1)
                        ge(act, "b_scores", 4 * tA - 4, 4 * B)
                        for c in range(NC):
                            last = act.activation(qT["b"][:, pA, c, :], m0[:, c * L:(c + 1) * L], ACT.Identity,
                                                  bias=bq_s[:, c:c + 1])
                        last.then_inc(s("b_queries"), 1)
                        ge(act, "c_umean", tA - 1)
                        act.activation(mean_v[:, pA, :], m0[:, 256:512], ACT.Copy).then_inc(s("a_mean"), 1)
                    if m == 4 and on(tC):
                        ge(act, "c_ctx_turned", tC + 1)
                        ge(act, "c_out", tC)
                        act.activation(ctxT[:, :, :], two(m1), ACT.Copy).then_inc(s("c_ctxT"), 1)
                    if m == 4 and on(tA):
                        ge(act, "a_k_turned", tA + 1)
                        ge(act, "b_keys", tA)
                        act.activation(kT[:, :, :], two(m0), ACT.Copy).then_inc(s("a_kT"), 1)
                    if m == 6 and on(tC):
                        ge(act, "e_projected", tC + 1)
                        ge(act, "d_keys", tC)
                        act.activation(xkT[:, :, :], two(m2), ACT.Relu).then_inc(s("e_kT"), 1)
                        ge(act, "d_pv", 4 * tC - 4, 4 * B)
                        act.activation(vh["d"][:, pC, :, 0:DH], m2[:, 256:512].rearrange("p (h d) -> p h d", h=H),
                                       ACT.Relu).then_inc(s("d_values"), 1)
                    if m == 7 and on(tC):
                        ge(act, "c_xn_turned", tC + 1)
                        ge(act, "c_queried", tC)
                        act.activation(xn2T[:, :, :], two(m1), ACT.Copy).then_inc(s("c_xnT"), 1)
                    if on(q[m - 1][1]):
                        copy_T(*q[m - 1])
                    if on(q[m][1]):
                        exp(*q[m])
                    if m == 7 and on(tC):
                        ge(act, "c_queried", tC + 1)
                        ge(act, "d_scores", 4 * tC - 4, 4 * B)
                        act.activation(qT["d"][:, pC, :, :], two(m1), ACT.Relu).then_inc(s("d_queries"), 1)

            run_bodies(act, step)

            act.wait_ge(s("experts_in"), 16 * EXPERT_LOADS)
            def group(g):
                for c in range(NC):
                    ge(act, "f_turned", g * 2 + c + 1, ANY)
                    if c == 0:
                        ge(act, "f_h1_mm", g * 2 * NE, ANY)
                    act.activation(x3T[:, c, :], bank[6 + c][:, :], ACT.Copy).then_inc(s("f_x3T"), 1)
                ge(act, "f_shifted", g + 1, ANY)
                act.activation(pe_[:, :, :], lg[:, :, :], ACT.Exp).then_inc(s("f_exp"), 1)
                ge(act, "f_cw_turned", g + 1, ANY)
                act.activation(cwT[:, :, :], bank[7][0:NE, :].rearrange("p (t l) -> p t l", t=GT), ACT.Copy)\
                    .then_inc(s("f_cwT"), 1)
                for e in range(NE):
                    ge(act, "f_h1_mm", g * 2 * NE + 2 * e + 1, ANY)
                    ge(act, "f_h2_mm", g * 2 * NE + 2 * e, ANY)
                    act.activation(h1[:, 0, :], bank[0][:, :], ACT.Relu, bias=b1_s[:, e, 0:1]).then_inc(s("f_h1a"), 1)
                    ge(act, "f_h2_mm", g * 2 * NE + 2 * e + 1, ANY)
                    ge(act, "f_h3_done", g * 2 * NE + 2 * e, ANY)
                    act.activation(h2[:, 0, :], bank[2][:, :], ACT.Relu, bias=b2_s[:, e, 0:1]).then_inc(s("f_h2a"), 1)
                ge(act, "f_acc", g * (NE + 1) * 2 + (NE + 1) * 2, ANY)
                act.dma_start(out[bass.ds(g * GT, GT), :, :].rearrange("b p n -> p b n"),
                              xall[:, bass.ds(g * GT, GT), :]).then_inc(s("out_done"), 16)

            group(0)
            with act.Fori(1, NG) as g:
                group(g)

            act.wait_ge(s("out_done"), 16 * NG)

        def add_expert(dve, g, e):
            for hf in range(2):
                dve.wait_ge(s("f_h3_done"), g * 2 * NE + 2 * e + hf + 1)
                dve.wait_ge(s("f_acc"), g * 2 * (NE + 1) + 2 * e + hf + 1)
                for t in range(2):
                    a = xall[:, bass.ds(g * GT + 2 * hf + t, 1), :].rearrange("p b n -> p (b n)")
                    last = dve.scalar_tensor_tensor(a, bank[4 + hf][:, t * D:(t + 1) * D],
                                                    cw[:, 2 * hf + t, e:e + 1], a, ALU.mult, ALU.add)
                last.then_inc(s("f_acc"), 1)

        @block.vector
        def _(dve):
            dve.wait_ge(s("const_in"), 16 * CONST)
            dve.wait_ge(s("pool_const"), 1)
            dve.tensor_copy(idx_f[:, :], idx_i[:, :]).then_inc(s("idx"), 1)
            dve.wait_ge(s("idx"), 1)
            dve.tensor_scalar(idx_n[:, :], idx_f[:, :], 0.0, float(L), ALU.is_lt, ALU.mult).then_inc(s("idx"), 1)
            dve.wait_ge(s("idx"), 2)
            dve.tensor_tensor(idx_f[:, :], idx_f[:, :], idx_n[:, :], ALU.add).then_inc(s("idx"), 1)
            dve.wait_ge(s("idx"), 3)
            dve.tensor_scalar(idx_n[:, :], idx_f[:, :], 0.0, float(L - 1), ALU.max, ALU.min).then_inc(s("idx"), 1)
            dve.wait_ge(s("idx"), 4)
            dve.tensor_scalar(samp[:, 0:U], idx_n[:, :], kcol[:, 0:1], None, ALU.is_equal).then_inc(s("idx"), 1)
            dve.wait_ge(s("idx"), 5)
            dve.reduce_sum(smax[:, 0:1], samp[:, 0:U], AX).then_inc(s("idx"), 1)
            dve.wait_ge(s("idx"), 6)
            dve.tensor_scalar(samp[:, U:UM], smax[:, 0:1], 1.0 / U, None, ALU.mult).then_inc(s("samp_ready"), 1)

            def quad(k, t, g):
                S4 = ps_s[k][:, :].rearrange("p (j l) -> p j l", j=HQ)
                ge(dve, f"{k}_scores", 4 * t + g + 1, 4 * B)
                dve.reduce_max(mx[k][:, :], S4, AX).then_inc(s(f"{k}_max"), 1)
                ge(dve, f"{k}_max", 4 * t + g + 1, 4 * B)
                ge(dve, f"{k}_probsT", 4 * t + g, 4 * B)
                dve.tensor_tensor(pr[k][:, :, :], S4, mx[k][:, :].unsqueeze(2).to_broadcast([128, HQ, L]),
                                  ALU.subtract).then_inc(s(f"{k}_shifted"), 1)

            def stats(src, stt, ag, name, t):
                alone(dve)
                dve.bn_stats(stt[:, :], src).then_inc(s(f"{name}_stats"), 1)
                ge(dve, f"{name}_stats", t + 1)
                alone(dve)
                dve.bn_aggr(ag[:, :], stt[:, :]).then_inc(s(f"{name}_aggr"), 1)

            def tile(t):
                return xall[:, bass.ds(t, 1), :].rearrange("p b n -> p (b n)")

            def heads(ap):
                return ap.rearrange("p (h d) -> p h d", h=H)

            def step(u, i, par):
                q = quads(u)
                tA, pA, tC, pC, tG = u - 1, parity(par, 1), u - 3, parity(par, 3), u - 5
                j = i - 1
                topk = par == 1 and (not is_int(j) or 0 <= j < B // 2)
                for m in range(8):
                    if on(q[m][1]):
                        quad(*q[m])
                    if m == 0 and topk:
                        ge(dve, "k_turned", j + 1)
                        dve.tensor_copy(mT[0][:, :], m2[0:32, 0:L]).then_inc(s("k_mT"), 1)
                        ge(dve, "k_mT", j + 1)
                        for r in range(U // 8):
                            alone(dve)
                            dve.max(top8[:, :], mT[r % 2][:, :]).then_inc(s("k_max"), 1)
                            ge(dve, "k_max", j * 5 + r + 1, 1 << 20)
                            alone(dve)
                            dve.match_replace(mT[(r + 1) % 2][:, :], top8[:, :], mT[r % 2][:, :], GONE)\
                                .then_inc(s("k_taken"), 1)
                            ge(dve, "k_taken", j * 5 + r + 1, 1 << 20)
                    if m == 1 and topk:
                        alone(dve)
                        dve.max(top8[:, :], mT[0][:, :]).then_inc(s("k_max"), 1)
                        ge(dve, "k_max", j * 5 + 5, 1 << 20)
                        dve.tensor_copy(top2[:, 0:U % 8], top8[:, 0:U % 8]).then_inc(s("k_top2"), 1)
                        ge(dve, "k_top2", j + 1)
                        alone(dve)
                        dve.match_replace(mT[1][:, :], top2[:, :], mT[0][:, :], GONE).then_inc(s("k_taken"), 1)
                        ge(dve, "k_taken", j * 5 + 5, 1 << 20)
                        ge(dve, "k_sel_turned", j)
                        dve.tensor_scalar(selT[:, :], mT[1][:, :], GONE, None, ALU.is_equal).then_inc(s("k_selT"), 1)
                    if m == 1 and on(tA):
                        ge(dve, "a_kv", tA + 1)
                        ge(dve, "a_sampled", tA)
                        dve.tensor_tensor(ktok[:, :], m0[:, 0:D], bk_s[:, :], ALU.add).then_inc(s("a_ktok"), 1)
                        ge(dve, "b_pv", 4 * tA - 4, 4 * B)
                        dve.tensor_tensor(vh["b"][:, pA, :, 0:DH], heads(m0[:, D:2 * D]), heads(bv_s[:, :]), ALU.add)\
                            .then_inc(s("b_values"), 1)
                    if m == 2 and topk:
                        ge(dve, "k_sel_turned", j + 1)
                        ge(dve, "c_umean", 2 * j)
                        dve.tensor_copy(sel[:, :, :], m2[:, 0:32].rearrange("p (b h) -> p b h", b=2)).then_inc(s("k_sel1"), 1)
                        dve.tensor_scalar(nsel[:, :, :], m2[:, 0:32].rearrange("p (b h) -> p b h", b=2), -1.0, 1.0,
                                          ALU.mult, ALU.add).then_inc(s("k_sel"), 1)
                    if m == 2 and on(tC):
                        jC = (i - 1) if par else (i - 2)
                        O = m1[:, :].rearrange("p (h e) -> p h e", h=H)
                        ge(dve, "c_oT_turned", tC + 1)
                        dve.reciprocal(rden[:, :], O[:, :, DH]).then_inc(s("c_rden"), 1)
                        ge(dve, "c_rden", tC + 1)
                        ge(dve, "k_sel", jC + 1)
                        dve.tensor_tensor(wsel[:, :], rden[:, :], sel[:, pC, :], ALU.mult).then_inc(s("c_wsel"), 1)
                        ge(dve, "c_wsel", tC + 1)
                        dve.tensor_tensor(heads(ctxa[:, :]), O[:, :, 0:DH],
                                          wsel[:, :].unsqueeze(2).to_broadcast([128, H, DH]), ALU.mult)\
                            .then_inc(s("c_scaled"), 1)
                        ge(dve, "c_scaled", tC + 1)
                        ge(dve, "c_umean", tC + 1)
                        ge(dve, "c_ctx_turned", tC)
                        dve.tensor_tensor(ctxv[:, :], ctxa[:, :], umean[:, :], ALU.add).then_inc(s("c_context"), 1)
                    if m == 3 and on(tG):
                        O = m2[:, :].rearrange("p (h e) -> p h e", h=H)
                        ge(dve, "g_oT_turned", tG + 1)
                        dve.reciprocal(xrden[:, :], O[:, :, DH]).then_inc(s("g_rden"), 1)
                        ge(dve, "g_rden", tG + 1)
                        dve.tensor_tensor(heads(xatt[:, :]), O[:, :, 0:DH],
                                          xrden[:, :].unsqueeze(2).to_broadcast([128, H, DH]), ALU.mult)\
                            .then_inc(s("g_scaled"), 1)
                        ge(dve, "g_scaled", tG + 1)
                        dve.tensor_tensor(tile(tG), xatt[:, :], tile(tG), ALU.add).then_inc(s("g_x2"), 1)
                    if m == 4 and on(tC):
                        ge(dve, "c_out", tC + 1)
                        ge(dve, "c_xb", tC + 1)
                        dve.tensor_tensor(tile(tC), m1[:, 0:D], tile(tC), ALU.add).then_inc(s("c_x1"), 1)
                        ge(dve, "c_x1", tC + 1)
                        stats(tile(tC), stc, agc, "c", tC)
                    if m == 5 and on(tA):
                        ge(dve, "a_sampled", tA + 1)
                        if is_int(tA) and tA == 0:
                            pass
                        ge(dve, "a_scored", tA)
                        dve.tensor_tensor(ksbd[:, :, :, :],
                                          m0[:, 0:NC * UM].rearrange("p (c u) -> p c u", c=NC).unsqueeze(2)
                                          .to_broadcast([128, NC, HQ, UM]),
                                          hmask[:, :].unsqueeze(1).unsqueeze(3).to_broadcast([128, NC, HQ, UM]),
                                          ALU.mult).then_inc(s("a_ksbd"), 1)
                    if m == 5 and on(tC):
                        ge(dve, "c_rstd", tC + 1)
                        ge(dve, "c_aggr", tC + 1)
                        ge(dve, "c_xn_turned", tC)
                        dve.tensor_scalar(xn2[:, :], tile(tC), agc[:, 0:1], rsc[:, 1:2], ALU.subtract, ALU.mult)\
                            .then_inc(s("c_xn"), 1)
                    if m == 5 and on(u):
                        ge(dve, f"x_in{par}", i * 16 + 16, 16 * B)
                        ge(dve, "l_rstd", u)
                        stats(tile(u), stl, agl, "l", u)
                    if m == 6 and on(u):
                        ge(dve, "l_rstd", u + 1)
                        ge(dve, "l_aggr", u + 1)
                        ge(dve, "a_transposed", u - 1)
                        dve.tensor_scalar(xn[:, par, :], tile(u), agl[:, 0:1], rsl[:, 1:2], ALU.subtract, ALU.mult)\
                            .then_inc(s("l_xn"), 1)
                    if m == 7 and on(tA):
                        ge(dve, "a_scored", tA + 1)
                        W4 = smax[:, :].rearrange("p (c r j) -> p c r j", c=NC, r=2)
                        V4 = mtok[:, pA, :].rearrange("p (c r j) -> p c r j", c=NC, r=2)
                        SS = [mm[:, 0:NC * HQ * UM].rearrange("p (c j u) -> p c j u", c=NC, j=HQ) for mm in (m0, m2)]
                        for r in range(2):
                            dve.reduce_max(W4[:, :, r, :], SS[r][:, :, :, 0:U], AX).then_inc(s("a_smax"), 1)
                        ge(dve, "a_smax", tA * 2 + 2, 2 * B)
                        ge(dve, "k_turned", (i - 1) if par else (i - 1), B // 2)
                        for r in range(2):
                            last = dve.tensor_tensor(V4[:, :, r, :], W4[:, :, r, :], SS[r][:, :, :, U], ALU.subtract)
                            last.then_inc(s("a_m"), 1)

            run_bodies(dve, step)

            dve.wait_ge(s("experts_in"), 16 * EXPERT_LOADS)
            def group(g):
                xg = xall[:, bass.ds(g * GT, GT), :]
                for t in range(GT):
                    dve.bn_stats(st3[:, t, :], xall[:, bass.ds(g * GT + t, 1), :].rearrange("p b n -> p (b n)"))\
                        .then_inc(s("f_stats"), 1)
                ge(dve, "f_stats", g * GT + GT, ANY)
                alone(dve)
                for t in range(GT):
                    last = dve.bn_aggr(ag3[:, t, :], st3[:, t, :])
                last.then_inc(s("f_aggr"), 1)
                ge(dve, "f_rstd", g + 1, ANY)
                ge(dve, "f_aggr", g + 1, ANY)
                ge(dve, "f_turned", g * 2, ANY)
                for t in range(GT):
                    last = dve.tensor_scalar(xn3[:, t, :], xall[:, bass.ds(g * GT + t, 1), :].rearrange("p b n -> p (b n)"),
                                             ag3[:, t, 0:1], rs3[:, 1, t:t + 1], ALU.subtract, ALU.mult)
                last.then_inc(s("f_xn"), 1)
                ge(dve, "f_gate", g + 1, ANY)
                lgp = bank[7][:, 0:GT * NE].rearrange("p (t e) -> p t e", t=GT)
                dve.tensor_tensor(lg[:, :, :], lgp, gb_s[:, :].unsqueeze(1).to_broadcast([128, GT, NE]), ALU.add)\
                    .then_inc(s("f_lg"), 1)
                ge(dve, "f_lg", g + 1, ANY)
                dve.reduce_max(gm[:, :], lg[:, :, :], AX).then_inc(s("f_gm"), 1)
                ge(dve, "f_gm", g + 1, ANY)
                dve.tensor_tensor(lg[:, :, :], lg[:, :, :], gm[:, :].unsqueeze(2).to_broadcast([128, GT, NE]), ALU.subtract)\
                    .then_inc(s("f_shifted"), 1)
                ge(dve, "f_exp", g + 1, ANY)
                dve.reduce_sum(gm[:, :], pe_[:, :, :], AX).then_inc(s("f_gsum"), 1)
                ge(dve, "f_gsum", g + 1, ANY)
                dve.reciprocal(gs[:, :], gm[:, :]).then_inc(s("f_grec"), 1)
                ge(dve, "f_grec", g + 1, ANY)
                dve.tensor_tensor(lg[:, :, :], pe_[:, :, :], gs[:, :].unsqueeze(2).to_broadcast([128, GT, NE]), ALU.mult)\
                    .then_inc(s("f_p"), 1)
                ge(dve, "f_p", g + 1, ANY)
                alone(dve)
                for t in range(GT):
                    last = dve.max(pt8[:, t, :], lg[:, t, :])
                last.then_inc(s("f_top"), 1)
                ge(dve, "f_top", g + 1, ANY)
                alone(dve)
                for t in range(GT):
                    last = dve.max_index(pi8[:, t, :], pt8[:, t, :], lg[:, t, :])
                last.then_inc(s("f_ti"), 1)
                ge(dve, "f_ti", g + 1, ANY)
                dve.tensor_copy(pf8[:, :, :], pi8[:, :, :]).then_inc(s("f_tf"), 1)
                ge(dve, "f_tf", g + 1, ANY)
                for t in range(GT):
                    dve.tensor_scalar(oh0[:, t, :], iota8[:, :], pf8[:, t, 0:1], lg[:, t, 0:1], ALU.is_equal, ALU.mult)
                    last = dve.tensor_scalar(cw[:, t, :], iota8[:, :], pf8[:, t, 1:2], lg[:, t, 1:2], ALU.is_equal, ALU.mult)
                last.then_inc(s("f_oh"), 1)
                ge(dve, "f_oh", g + 1, ANY)
                dve.tensor_tensor(cw[:, :, :], cw[:, :, :], oh0[:, :, :], ALU.add).then_inc(s("f_cw"), 1)
                for hf in range(2):
                    ge(dve, "f_b3", g * 2 + hf + 1, ANY)
                    dve.tensor_tensor(xall[:, bass.ds(g * GT + 2 * hf, 2), :],
                                      bank[4 + hf][:, :].rearrange("p (t n) -> p t n", t=2),
                                      xall[:, bass.ds(g * GT + 2 * hf, 2), :], ALU.add).then_inc(s("f_acc"), 1)
                for e in range(NE):
                    ge(dve, "f_h1_mm", g * 2 * NE + 2 * e + 2, ANY)
                    ge(dve, "f_h2_mm", g * 2 * NE + 2 * e, ANY)
                    dve.tensor_scalar(h1[:, 1, :], bank[1][:, :], b1_s[:, e, 1:2], 0.0, ALU.add, ALU.max).then_inc(s("f_h1b"), 1)
                    ge(dve, "f_h2_mm", g * 2 * NE + 2 * e + 2, ANY)
                    ge(dve, "f_h3_done", g * 2 * NE + 2 * e, ANY)
                    dve.tensor_scalar(h2[:, 1, :], bank[3][:, :], b2_s[:, e, 1:2], 0.0, ALU.add, ALU.max).then_inc(s("f_h2b"), 1)
                    if e >= 1:
                        add_expert(dve, g, e - 1)
                add_expert(dve, g, NE - 1)

            group(0)
            with dve.Fori(1, NG) as g:
                group(g)

        @block.tensor
        def _(pe):
            mm = nc.tensor.matmul

            def scores(k, t, g, p):
                c, r = g // 2, g % 2
                rows = slice(64 * r, 64 * r + 64)
                if g == 0:
                    ge(pe, f"{k}_queries", t + 1)
                    ge(pe, f"{k}_keys", t + 1)
                ge(pe, f"{k}_shifted", 4 * t + g, 4 * B)
                mm(ps_s[k][:, :], qT[k][rows, p, c, :], kbd[k][rows, p, c, :, :].rearrange("p j l -> p (j l)"),
                   start=True, stop=True).then_inc(s(f"{k}_scores"), 1)

            def turn_probs(k, t, g, u):
                ge(pe, f"{k}_probs", 4 * t + g + 1, 4 * B)
                if k == "b":
                    ge(pe, "d_prT", 4 * (u - 4) + g, 4 * B)
                    if is_int(t):
                        ge(pe, "b_prT", 4 * t + g, 4 * B)
                else:
                    ge(pe, "b_prT", 4 * (u - 2) + g + 1 if g < 3 else 4 * (u - 3) + 4, 4 * B)
                    if is_int(t):
                        ge(pe, "d_prT", 4 * t + g, 4 * B)
                for j in range(HQ):
                    last = nc.tensor.transpose(ps_at[:, j * L:(j + 1) * L], pr[k][:, j, :], ident[:, :])
                last.then_inc(s(f"{k}_probsT"), 1)

            def pv(k, t, g, p):
                ge(pe, f"{k}_prT", 4 * t + g + 1, 4 * B)
                if g == 0:
                    ge(pe, f"{k}_values", t + 1)
                    ge(pe, f"{k}_oT", t)
                for j in range(HQ):
                    last = mm(ps_o[k][HS * j:HS * j + HS, g * L:(g + 1) * L], vh[k][:, p, HQ * g + j, :], prT[k][:, j, :],
                              start=True, stop=True, skip_group_check=True)
                last.then_inc(s(f"{k}_pv"), 1)

            def turn(dst, src, n=NC):
                for c in range(n):
                    last = nc.tensor.transpose(dst[:, c * L:(c + 1) * L], src[:, c * 128:(c + 1) * 128], ident[:, :])
                return last

            def rows_out(dst, w, src):
                for c in range(NC):
                    for k in range(NC):
                        last = mm(dst[:, c * L:(c + 1) * L], w[:, k, c * 128:(c + 1) * 128], src[:, k, :],
                                  start=(k == 0), stop=(k == NC - 1))
                return last

            pe.wait_ge(s("const_in"), 16 * CONST)
            pe.wait_ge(s("pool_const"), 1)
            pe.wait_ge(s("samp_ready"), 1)

            def step(u, i, par):
                q = quads(u)
                tA, pA, tC, pC, tG = u - 1, parity(par, 1), u - 3, parity(par, 3), u - 5
                j = i - 1
                topk = par == 1 and (not is_int(j) or 0 <= j < B // 2)
                for m in range(8):
                    for back, what in ((0, "s"), (1, "t"), (2, "v")):
                        k, t, g = q[m - back]
                        if not on(t):
                            continue
                        p = par if m - back >= 0 else 1 - par
                        if what == "s":
                            scores(k, t, g, p)
                        elif what == "t":
                            turn_probs(k, t, g, u)
                        else:
                            pv(k, t, g, p)
                    if m == 0 and on(tA):
                        ge(pe, "l_xn", tA + 1)
                        ge(pe, "a_m", 2 * tA, 2 * B)
                        turn(m0, xn[:, pA, :]).then_inc(s("a_transposed"), 1)
                    if m == 0 and topk:
                        ge(pe, "a_m", j * 4 + 4, 2 * B)
                        nc.tensor.transpose(m2[0:32, 0:L], mtok[:, :, :].rearrange("p b h -> p (b h)"), ident[:, :])\
                            .then_inc(s("k_turned"), 1)
                    if m == 1 and on(tC):
                        ge(pe, "b_oT", tC + 1)
                        ge(pe, "d_queries", tC)
                        turn(m1, oT["b"][:, :, :].rearrange("p g l -> p (g l)"), NQ).then_inc(s("c_oT_turned"), 1)
                    if m == 1 and on(tC):
                        jC = (i - 1) if par else (i - 2)
                        ge(pe, f"ctx_in{pC}", jC * 16 + 16, 16 * B)
                        ge(pe, "a_m", 2 * (u - 1), 2 * B)
                        if topk:
                            ge(pe, "k_mT", j + 1)
                        turn(m2, cin[:, pC, :]).then_inc(s("e_transposed"), 1)
                    if m == 1 and on(tA):
                        ge(pe, "a_xnT", tA + 1)
                        for k in range(NC):
                            last = mm(m0[:, :], xnT[:, k, :], wkv_s[:, k, :], start=(k == 0), stop=(k == NC - 1))
                        last.then_inc(s("a_kv"), 1)
                    if m == 2 and topk:
                        ge(pe, "k_selT", j + 1)
                        ge(pe, "e_cT", tC + 1)
                        alone(pe)
                        nc.tensor.transpose(m2[:, 0:32], selT[:, :], ident[0:32, 0:32]).then_inc(s("k_sel_turned"), 1)
                    if m == 2 and on(tA):
                        ge(pe, "a_ktok", tA + 1)
                        ge(pe, "b_values", tA + 1)
                        rows_out(m0, wq_s, xnT)
                        mm(m0[:, 256:512].rearrange("p (h d) -> p h d", h=H), mean_w[:, :], vh["b"][:, pA, :, 0:DH],
                           start=True, stop=True).then_inc(s("a_projected"), 1)
                    if m == 3 and on(tC):
                        ge(pe, "c_context", tC + 1)
                        turn(m1, ctxv).then_inc(s("c_ctx_turned"), 1)
                    if m == 3 and on(tG):
                        ge(pe, "d_oT", tG + 1)
                        ge(pe, "e_cT", tC + 1)
                        if topk:
                            ge(pe, "k_sel", j + 1)
                        turn(m2, oT["d"][:, :, :].rearrange("p g l -> p (g l)"), NQ).then_inc(s("g_oT_turned"), 1)
                    if m == 3 and on(tA):
                        ge(pe, "b_queries", tA + 1)
                        ge(pe, "a_mean", tA + 1)
                        turn(m0, ktok).then_inc(s("a_k_turned"), 1)
                    if m == 4 and on(tC):
                        ge(pe, "c_ctxT", tC + 1)
                        for k in range(NC):
                            last = mm(m1[:, 0:D], ctxT[:, k, :], wo_s[:, k, :], start=(k == 0), stop=(k == NC - 1))
                        last.then_inc(s("c_out"), 1)
                    if m == 5 and on(tC):
                        ge(pe, "g_scaled", tG + 1)
                        ge(pe, "e_cT", tC + 1)
                        if topk:
                            ge(pe, "k_sel", j + 1)
                        rows_out(m2, xwk_s, cT)
                        for k in range(NC):
                            last = mm(m2[:, 256:512], cT[:, k, :], xwv_s[:, k, :], start=(k == 0), stop=(k == NC - 1))
                        last.then_inc(s("e_projected"), 1)
                    if m == 5 and on(tA):
                        ge(pe, "a_kT", tA + 1)
                        for c in range(NC):
                            last = mm(m0[:, c * UM:(c + 1) * UM], ktok[:, c * 128:(c + 1) * 128], samp[:, :],
                                      start=True, stop=True)
                        last.then_inc(s("a_sampled"), 1)
                    if m == 6 and on(tC):
                        ge(pe, "c_xn", tC + 1)
                        turn(m1, xn2).then_inc(s("c_xn_turned"), 1)
                    if m == 7 and on(tC):
                        ge(pe, "c_xnT", tC + 1)
                        rows_out(m1, xwq_s, xn2T).then_inc(s("c_queried"), 1)
                    if m == 7 and on(tA):
                        ge(pe, "a_ksbd", tA + 1)
                        ge(pe, "e_kT", tC + 1)
                        ge(pe, "d_values", tC + 1)
                        ge(pe, "g_scaled", tG + 1)
                        if topk:
                            ge(pe, "k_sel", j + 1)
                        for c in range(NC):
                            for r in range(2):
                                rows = slice(64 * r, 64 * r + 64)
                                last = mm((m0, m2)[r][:, c * HQ * UM:(c + 1) * HQ * UM], qT["b"][rows, pA, c, :],
                                          ksbd[rows, c, :, :].rearrange("p j u -> p (j u)"), start=True, stop=True)
                        last.then_inc(s("a_scored"), 1)

            run_bodies(pe, step)

            pe.wait_ge(s("experts_in"), 16 * EXPERT_LOADS)

            def group(g):
                ge(pe, "f_xn", g + 1, ANY)
                for c in range(NC):
                    if c == 1:
                        ge(pe, "f_cwT", g, ANY)
                    for t in range(GT):
                        last = nc.tensor.transpose(bank[6 + c][:, t * L:(t + 1) * L], xn3[:, t, c * 128:(c + 1) * 128], ident[:, :])
                    last.then_inc(s("f_turned"), 1)
                ge(pe, "f_x3T", g * 2 + 2, ANY)
                for t in range(GT):
                    for k in range(NC):
                        last = mm(bank[7][:, t * NE:(t + 1) * NE], x3T[:, k, t * L:(t + 1) * L], gw_s[:, k, :],
                                  start=(k == 0), stop=(k == NC - 1))
                last.then_inc(s("f_gate"), 1)

                def l1(e):
                    for c in range(NC):
                        ge(pe, ("f_h1a", "f_h1b")[c], g * NE + e, ANY)
                        for k in range(NC):
                            last = mm(bank[c][:, :], w_s[0][:, e, k, c * 128:(c + 1) * 128], x3T[:, k, :],
                                      start=(k == 0), stop=(k == NC - 1))
                        last.then_inc(s("f_h1_mm"), 1)

                def l2(e):
                    ge(pe, "f_h1a", g * NE + e + 1, ANY)
                    ge(pe, "f_h1b", g * NE + e + 1, ANY)
                    for c in range(NC):
                        ge(pe, ("f_h2a", "f_h2b")[c], g * NE + e, ANY)
                        for k in range(NC):
                            last = mm(bank[2 + c][:, :], w_s[1][:, e, k, c * 128:(c + 1) * 128], h1[:, k, :],
                                      start=(k == 0), stop=(k == NC - 1))
                        last.then_inc(s("f_h2_mm"), 1)

                def l3(e):
                    ge(pe, "f_h2a", g * NE + e + 1, ANY)
                    ge(pe, "f_h2b", g * NE + e + 1, ANY)
                    for hf in range(2):
                        ge(pe, "f_acc", g * 2 * (NE + 1) + 2 * e + hf + 1, ANY)
                        for t in range(2):
                            for k in range(NC):
                                tt = 2 * hf + t
                                last = mm(bank[4 + hf][:, t * D:(t + 1) * D], h2[:, k, tt * L:(tt + 1) * L], w_s[2][:, e, k, :],
                                          start=(k == 0), stop=(k == NC - 1))
                        last.then_inc(s("f_h3_done"), 1)

                l1(0)
                ge(pe, "f_cw", g + 1, ANY)
                for t in range(GT):
                    last = nc.tensor.transpose(bank[7][0:NE, t * L:(t + 1) * L], cw[:, t, :], ident[:, :])
                last.then_inc(s("f_cw_turned"), 1)
                ge(pe, "f_cwT", g + 1, ANY)
                for hf in range(2):
                    ge(pe, "f_acc", g * 2 * (NE + 1), ANY)
                    for t in range(2):
                        last = mm(bank[4 + hf][:, t * D:(t + 1) * D], cwT[:, 2 * hf + t, :], b3_s[:, :], start=True, stop=True)
                    last.then_inc(s("f_b3"), 1)
                l2(0)
                for e in range(NE):
                    if e + 1 < NE:
                        l1(e + 1)
                    l3(e)
                    if e + 1 < NE:
                        l2(e + 1)

            group(0)
            with pe.Fori(1, NG) as g:
                group(g)

_OUT = ((B, L, D), "float32")


def kernel(**inputs):
    import numpy as np
    import concourse.bacc as bacc
    from concourse import mybir as mb
    from concourse.bass_utils import run_bass_kernel_spmd

    a = {k: np.ascontiguousarray(v) for k, v in inputs.items()}
    p = "L0_attn_"
    f = "L0_ffn_"
    data = {"x": a["x"], "ctx": a["ctx_1024"], "wq": a[p + "W_q"], "bq": a[p + "b_q"], "wk": a[p + "W_k"],
            "bk": a[p + "b_k"], "wv": a[p + "W_v"], "bv": a[p + "b_v"], "wo": a[p + "W_o"], "bo": a[p + "b_o"],
            "sidx": a[p + "k_sample_idx"],
            "xwqT": np.ascontiguousarray(a["L0_xattn_Wq"].T), "xwkT": np.ascontiguousarray(a["L0_xattn_Wk"].T),
            "xwvT": np.ascontiguousarray(a["L0_xattn_Wv"].T),
            "gwT": np.ascontiguousarray(a[f + "gate_w"].T), "gb": a[f + "gate_b"],
            "w1": a[f + "w1"], "b1": a[f + "b1"], "w2": a[f + "w2"], "b2": a[f + "b2"], "w3": a[f + "w3"],
            "b3": a[f + "b3"],
            "ident_d": np.eye(128, dtype=np.float32),
            "hmask_d": (np.arange(128)[:, None] % 64 // 16 == np.arange(4)[None, :]).astype(np.float32),
            "iota8_d": np.tile(np.arange(8, dtype=np.float32), (128, 1)),
            "kcol_d": np.arange(128, dtype=np.float32)[:, None]}
    nc = bacc.Bacc("TRN2", target_bir_lowering=False, num_devices=1)
    arrays, args = {}, []
    for name, v in data.items():
        arrays[f"in_{name}"] = v
        args.append(nc.dram_tensor(f"in_{name}", v.shape, mb.dt.from_np(v.dtype), kind="ExternalInput").ap())
    args.append(nc.dram_tensor("out_0", _OUT[0], mb.dt.float32, kind="ExternalOutput").ap())
    decoder_block(nc, *args)
    r = run_bass_kernel_spmd(nc, [arrays], core_ids=[0])
    return r.results[0]["out_0"]
```

```python
import concourse.bass as bass
from concourse import mybir
from contextlib import ExitStack

B, L, D, H, U, NE = 64, 128, 256, 16, 34, 8
DH = D // H
NC = D // 128
HQ = 4
NQ = H // HQ
UM = U + 1
HS = 32
TS = 4
TR = TS * 128
NT = B * L * 2 // TR + NE - 1
RC = B * L + TR
RW = D + 1
NOWHERE = float(4 * B * L)
WL = NC * D
WP = 3 * WL + 2 * NC
TB = 3
GT = 4
NG = B // GT
EPS = 1e-5
GONE = -3.0e38


def decoder_block(nc, x, ctx, wq, bq, wk, bk, wv, bv, wo, bo, sidx, xwqT, xwkT, xwvT,
                  gwT, gb, experts, b3, ident_d, hmask_d, iota8_d, kcol_d, tri_d, token_d, row0_d,
                  steps_d, upto_d, tiles_d, out):
    f32, i32, u32 = mybir.dt.float32, mybir.dt.int32, mybir.dt.uint32
    bf16 = mybir.dt.bfloat16
    ALU, ACT, AX = mybir.AluOpType, mybir.ActivationFunctionType, mybir.AxisListType.X

    st = ExitStack()
    with st:
        def sb(name, shape, dt=f32):
            return st.enter_context(nc.sbuf_tensor(name, shape, dt))

        def sem(name):
            return st.enter_context(nc.semaphore(name))

        bank = [st.enter_context(nc.psum_tensor(f"bank{i}", [128, 512], f32)) for i in range(8)]
        ps_s = {"b": bank[0], "d": bank[1]}
        ps_at = bank[2]
        ps_o = {"b": bank[3], "d": bank[4]}
        m0, m1, m2 = bank[5], bank[6], bank[7]

        ident = sb("ident", [128, 128])
        hmask = sb("hmask", [128, HQ])
        iota8 = sb("iota8", [128, NE])
        kcol = sb("kcol", [128, 1])
        mean_w = sb("mean_w", [128, 128])
        epsc = sb("epsc", [128, 1])
        mhalf = sb("mhalf", [128, 1])
        wq_s, wo_s = sb("wq_s", [128, NC, D]), sb("wo_s", [128, NC, D])
        wkv_s = sb("wkv_s", [128, NC, 2 * D])
        xwq_s, xwk_s, xwv_s = (sb(n, [128, NC, D]) for n in ("xwq_s", "xwk_s", "xwv_s"))
        bq_s = sb("bq_s", [128, NC])
        bk_s, bv_s, bo_s = (sb(n, [128, D]) for n in ("bk_s", "bv_s", "bo_s"))
        idx_i, idx_f, idx_n = sb("idx_i", [128, U], i32), sb("idx_f", [128, U]), sb("idx_n", [128, U])
        samp = sb("samp", [128, UM])
        gw_s, gb_s = sb("gw_s", [128, NC, NE]), sb("gb_s", [NE, 1])
        tri_f, tri = sb("tri_f", [128, 128]), sb("tri", [128, 128], bf16)
        ones = sb("ones", [128, 128], bf16)
        token = sb("token", [128, B, 2])
        row0 = sb("row0", [128, NE])
        steps_c = sb("steps_c", [128, B * L // TR])
        upto = sb("upto", [128, NE, NE])
        tile_c = sb("tile_c", [128, NT])

        xall = sb("xall", [128, B, D])

        xn = sb("xn", [128, 2, D])
        xnT = sb("xnT", [128, NC, L])
        ktok = sb("ktok", [128, D])
        kT = sb("kT", [128, NC, L])
        qT = {"b": sb("qT", [128, 2, NC, L]), "d": sb("xqT", [128, 2, NC, L])}
        kbd = {"b": sb("kbd", [128, 2, NC, HQ, L]), "d": sb("xkbd", [128, 2, NC, HQ, L])}
        vh = {"b": sb("vh", [128, 2, H, HS]), "d": sb("xvh", [128, 2, H, HS])}
        mean_v = sb("mean_v", [128, 2, D])
        ksbd = sb("ksbd", [128, NC, HQ, UM])
        smax = sb("smax", [128, H])
        mtok = sb("mtok", [128, 2, H])
        mT = [sb("mT0", [32, L]), sb("mT1", [32, L])]
        top8 = sb("top8", [32, 8])
        top2 = sb("top2", [32, 8])
        selT = sb("selT", [32, L])
        sel, nsel = sb("sel", [128, 2, H]), sb("nsel", [128, 2, H])
        mx = {"b": sb("mx", [128, HQ]), "d": sb("xmx", [128, HQ])}
        pr = {"b": sb("pr", [128, HQ, L]), "d": sb("xpr", [128, HQ, L])}
        prT = {"b": sb("prT", [128, HQ, L]), "d": sb("xprT", [128, HQ, L])}
        oT = {"b": sb("oT", [128, NQ, L]), "d": sb("xoT", [128, NQ, L])}
        rden, wsel = sb("rden", [128, H]), sb("wsel", [128, H])
        xrden = sb("xrden", [128, H])
        ctxa, ctxv, umean = sb("ctxa", [128, D]), sb("ctxv", [128, D]), sb("umean", [128, D])
        ctxT = sb("ctxT", [128, NC, L])
        xn2, xn2T = sb("xn2", [128, D]), sb("xn2T", [128, NC, L])
        xatt = sb("xatt", [128, D])
        cin = sb("cin", [128, 2, D])
        cT, xkT = sb("cT", [128, NC, L]), sb("xkT", [128, NC, L])
        stl, agl, rsl = sb("stl", [128, 6]), sb("agl", [128, 2]), sb("rsl", [128, 2])
        stc, agc, rsc = sb("stc", [128, 6]), sb("agc", [128, 2]), sb("rsc", [128, 2])

        stf, agf, vef = sb("stf", [128, 6]), sb("agf", [128, 2]), sb("vef", [128, 1])
        norm3 = sb("norm3", [128, B, 2])
        xn3, x3p = sb("xn3", [128, 2, D]), sb("x3p", [128, NC, 2 * L])
        lgT = sb("lgT", [NE, 2 * L])
        lg, pe_ = sb("lg", [128, 2, NE]), sb("pe_", [128, 2, NE])
        gm, gs, gr = sb("gm", [128, 2]), sb("gs", [128, 2]), sb("gr", [128, 2])
        probs = sb("probs", [128, 2, NE])
        pt8, pi8 = sb("pt8", [128, 2, 8]), sb("pi8", [128, 2, 8], u32)
        pf2 = sb("pf2", [128, 2, 2])
        oh = sb("oh", [128, 2, 2, NE])
        both = sb("both", [128, 2, NE], bf16)
        before = sb("before", [128, 2, NE], bf16)
        chosen = sb("chosen", [128, NE], bf16)
        posE, ohp = sb("posE", [128, 2, NE]), sb("ohp", [128, 2, 2, NE])
        slot_f, slot = sb("slot_f", [128, 2, 2]), sb("slot", [128, 2, 2], u32)
        xrow = sb("xrow", [128, 2, 2, RW])
        weigh = sb("weigh", [128, B, 2])

        cnt, nt, cum = sb("cnt", [128, NE]), sb("nt", [128, NE]), sb("cum", [128, NE])
        cmpS = sb("cmpS", [128, NE, B * L // TR])
        ntm = sb("ntm", [128, NE, NE])
        last1, ti = sb("last1", [128, 1]), sb("ti", [128, NT])
        cmpT, cmpN = sb("cmpT", [128, NT, NE]), sb("cmpN", [128, NT, NE])
        te, tn, trow = sb("te", [128, NT]), sb("tn", [128, NT]), sb("trow", [128, NT])
        te_i, trow_i = sb("te_i", [128, NT], i32), sb("trow_i", [128, NT], i32)
        pad0, pad_i = sb("pad0", [128, NE]), sb("pad_i", [128, NE], i32)
        padrow = sb("padrow", [128, TS, RW])

        wt = sb("wt", [128, TB, WP])
        b3r = sb("b3r", [128, TB, D])
        xs = sb("xs", [128, TB, TS, RW])
        x3T = [prT[k][:, :, :].rearrange("p j l -> p (j l)") for k in "bd"]
        h1, h2 = (vh[k][:, :, :, :].rearrange("p c h e -> p c (h e)") for k in "bd")
        y01 = sb("y01", [128, 2, TS, D])
        y = [y01[:, 0, :, :], y01[:, 1, :, :],
             xrow[:, :, :, :].rearrange("p b k r -> p (b k r)")[:, :TS * D].rearrange("p (t n) -> p t n", t=TS)]
        dest = sb("dest", [128, TB, TS], u32)
        yt = [kbd[k][:, :, :, :, :].rearrange("p k c j l -> p k (c j l)").rearrange("p k (t n) -> p k t n", t=GT) for k in "bd"]

        rows_d = nc.dram_tensor("dispatched", ((NE * RC), RW), f32, kind="Internal").ap()
        y_d = nc.dram_tensor("results", (2 * B * L, D), f32, kind="Internal").ap()

        S = {}

        def s(name):
            if name not in S:
                S[name] = sem(name)
            return S[name]

        block = st.enter_context(nc.Block())

        STEPS = B + 8
        PRO, LAST = 5, B // 2
        BODIES = (STEPS + 1) // 2

        ANY = 1 << 20

        def is_int(v):
            return isinstance(v, int)

        def on(t):
            return not is_int(t) or 0 <= t < B

        def on2(j):
            return not is_int(j) or 0 <= j < B // 2

        def ge(eng, name, v, most=B):
            if is_int(v):
                v = min(v, most)
                if v <= 0:
                    return
            eng.wait_ge(s(name), v)

        def alone(eng):
            eng.sem_inc(s("passed"), 1)

        def run_bodies(eng, step):
            for i in range(PRO):
                for par in range(2):
                    step(2 * i + par, i, par)
            with eng.Fori(PRO, LAST) as i:
                for par in range(2):
                    step(i * 2 + par, i, par)
            for i in range(LAST, BODIES):
                for par in range(2):
                    step(2 * i + par, i, par)

        def tiles_in(i, q):
            return (i - q + TB) * 16

        def results(g, q):
            return g * 16 + (16 if q else 32)

        def run_tiles(eng, body, ahead=0):
            for i in range(2 * TB):
                body(i, i % TB)
            with eng.Fori(2 * TB, NT - TB - TB * ahead + 1, TB) as i:
                for q in range(TB):
                    body(i + q, q)
            for i in range(NT - TB * ahead, NT):
                body(i, i % TB)

        def run_groups(eng, body):
            for g in range(2):
                body(g, g)
            with eng.Fori(2, NG - 1, 2) as g:
                body(g, 0)
                body(g + 1, 1)

        def quads(u):
            return {-2: ("b", u - 3, 3), -1: ("d", u - 5, 3),
                    **{2 * g: ("b", u - 2, g) for g in range(NQ)},
                    **{2 * g + 1: ("d", u - 4, g) for g in range(NQ)}}

        def parity(par, back):
            return (par + back) % 2

        @block.sync
        def _(sp):
            for dst, src in ((ident[:, :], ident_d), (hmask[:, :], hmask_d), (iota8[:, :], iota8_d),
                             (kcol[:, :], kcol_d), (tri_f[:, :], tri_d), (token[:, :, :], token_d), (row0[:, :], row0_d),
                             (steps_c[:, :], steps_d), (upto[:, :, :], upto_d), (tile_c[:, :], tiles_d)):
                sp.dma_start(dst, src).then_inc(s("const_in"), 16)
            for dst, src in ((wq_s, wq), (wo_s, wo)):
                sp.dma_start(dst[:, :, :], src.rearrange("(c p) n -> p c n", p=128)).then_inc(s("const_in"), 16)
            sp.dma_start(wkv_s[:, :, 0:D], wk.rearrange("(c p) n -> p c n", p=128)).then_inc(s("const_in"), 16)
            sp.dma_start(wkv_s[:, :, D:2 * D], wv.rearrange("(c p) n -> p c n", p=128)).then_inc(s("const_in"), 16)
            for dst, src in ((xwq_s, xwqT), (xwk_s, xwkT), (xwv_s, xwvT)):
                sp.dma_start(dst[:, :, :], src.rearrange("(c p) n -> p c n", p=128)).then_inc(s("const_in"), 16)
            with nc.allow_non_contiguous_dma(reason="small vectors, once"):
                sp.dma_start(bq_s[:, :], bq.rearrange("(c p) -> p c", p=128)).then_inc(s("const_in"), 16)
                sp.dma_start(gb_s[:, :], gb.rearrange("(n a) -> n a", a=1)).then_inc(s("const_in"), 16)
                sp.dma_start(gw_s[:, :, :], gwT.rearrange("(c p) n -> p c n", p=128)).then_inc(s("const_in"), 16)
                for dst, src, n in ((bk_s, bk, D), (bv_s, bv, D), (bo_s, bo, D), (idx_i, sidx, U)):
                    sp.dma_start(dst[:, :], src.rearrange("(a n) -> a n", a=1).to_broadcast([128, n])).then_inc(s("const_in"), 16)

            def step(u, i, par):
                if on(u):
                    ge(sp, f"x_in{par}", i * 16, 16 * B)
                    alone(sp)
                    sp.dma_start(xall[:, bass.ds(u, 1), :], x[bass.ds(u, 1), :, :].rearrange("b p n -> p b n"))\
                        .then_inc(s(f"x_in{par}"), 16)
                t, j = u - 2, i - 1
                if on(t):
                    ge(sp, f"ctx_in{par}", j * 16, 16 * B)
                    alone(sp)
                    ge(sp, "e_transposed", t - 1)
                    alone(sp)
                    sp.dma_start(cin[:, par, :], ctx[bass.ds(t, 1), :, :].rearrange("b p n -> p (b n)"))\
                        .then_inc(s(f"ctx_in{par}"), 16)

            run_bodies(sp, step)

            sp.wait_ge(s("dispatched"), 16 * 2 * B)
            sp.wait_ge(s("t_table"), 1)
            for e in range(NE):
                row = sp.value_load(pad_i[0:1, e:e + 1], min_val=0, max_val=NE * RC - TR)
                sp.dma_start(rows_d[bass.ds(row, TR), :].rearrange("(p s) n -> p s n", s=TS), padrow[:, :, :])\
                    .then_inc(s("pads_out"), 16)
            sp.wait_ge(s("pads_out"), 16 * NE)

            def tile_in(i, q):
                if not is_int(i) or i >= TB:
                    ge(sp, "x_dest", i - TB + 1, ANY)
                    alone(sp)
                    ge(sp, "y_ready", (i - TB) * 2 + 2, ANY)
                    alone(sp)
                e = sp.value_load(te_i[0:1, bass.ds(i, 1)], min_val=0, max_val=NE - 1)
                row = sp.value_load(trow_i[0:1, bass.ds(i, 1)], min_val=0, max_val=NE * RC - TR)
                sp.dma_start(xs[:, q, :, :], rows_d[bass.ds(row, TR), :].rearrange("(p s) n -> p s n", s=TS))\
                    .then_inc(s(f"tile_in{q}"), 16)
                sp.dma_start(wt[:, q, :], experts[bass.ds(e, 1), :, :].rearrange("e p n -> p (e n)"))\
                    .then_inc(s(f"tile_in{q}"), 16)
                sp.dma_start(b3r[:, q, :], b3[bass.ds(e, 1), :].to_broadcast([128, D])).then_inc(s(f"tile_in{q}"), 16)

            run_tiles(sp, tile_in)

            sp.wait_ge(s("y_out"), 16 * TS * NT)

            def results_in(g, q):
                if not is_int(g) or g >= 2:
                    ge(sp, "added", g - 1, ANY)
                    alone(sp)
                for k in range(2):
                    sp.dma_start(yt[q][:, k, :, :],
                                 y_d[bass.ds(g * (GT * L) + k * B * L, GT * L), :].rearrange("(t p) n -> p t n", p=L))\
                        .then_inc(s(f"results_in{q}"), 16)

            run_groups(sp, results_in)

        CONST = 24

        @block.gpsimd
        def _(pool):
            pool.memset(mean_w[:, :], 1.0 / L)
            pool.memset(epsc[:, :], EPS)
            pool.memset(mhalf[:, :], -0.5)
            for k in "bd":
                pool.memset(vh[k][:, :, :, :], 0.0).then_inc(s("zeroed"), 1)
            pool.wait_ge(s("zeroed"), 2)
            for k in "bd":
                pool.memset(vh[k][:, :, :, DH:DH + 1], 1.0).then_inc(s("ones_set"), 1)
            pool.wait_ge(s("ones_set"), 2)
            pool.memset(ones[:, :], 1.0)
            pool.memset(chosen[:, :], 0.0)
            pool.memset(padrow[:, :, 0:D], 0.0)
            pool.memset(padrow[:, :, D:RW], NOWHERE)
            pool.memset(top2[:, :], GONE).then_inc(s("pool_const"), 1)
            pool.wait_ge(s("pool_const"), 1)

            def rstd(aggr, rs, name, t):
                ge(pool, f"{name}_aggr", t + 1)
                pool.tensor_tensor(rs[:, 0:1], aggr[:, 1:2], epsc[:, 0:1], ALU.add).then_inc(s(f"{name}_veps"), 1)
                ge(pool, f"{name}_veps", t + 1)
                pool.tensor_tensor(rs[:, 1:2], rs[:, 0:1], mhalf[:, 0:1], ALU.pow).then_inc(s(f"{name}_rstd"), 1)

            def blocks(k, src, name, t, p):
                ge(pool, f"{name}_kT", t + 1)
                ge(pool, f"{k}_scores", 4 * t - 4, 4 * B)
                pool.tensor_tensor(kbd[k][:, p, :, :, :],
                                   src[:, :, :].unsqueeze(2).to_broadcast([128, NC, HQ, L]),
                                   hmask[:, :].unsqueeze(1).unsqueeze(3).to_broadcast([128, NC, HQ, L]),
                                   ALU.mult).then_inc(s(f"{k}_keys"), 1)

            pool.wait_ge(s("const_in"), 16 * CONST)

            def step(u, i, par):
                t, p = u - 3, parity(par, 3)
                if on(t):
                    ge(pool, "l_xn", t + 1)
                    pool.tensor_tensor(xall[:, bass.ds(t, 1), :].rearrange("p b n -> p (b n)"),
                                       xall[:, bass.ds(t, 1), :].rearrange("p b n -> p (b n)"),
                                       bo_s[:, :], ALU.add).then_inc(s("c_xb"), 1)
                    j = (i - 1) if par else (i - 2)
                    ge(pool, "k_sel", j + 1)
                    ge(pool, "a_mean", t + 1)
                    ge(pool, "c_context", t)
                    pool.tensor_tensor(umean[:, :].rearrange("p (h d) -> p h d", h=H),
                                       mean_v[:, p, :].rearrange("p (h d) -> p h d", h=H),
                                       nsel[:, p, :].unsqueeze(2).to_broadcast([128, H, DH]),
                                       ALU.mult).then_inc(s("c_umean"), 1)
                j = i - 4
                if par == 0 and on2(j):
                    ge(pool, "f_both", j + 1)
                    ge(pool, "f_pos", j)
                    ge(pool, "f_chosen", j)
                    alone(pool)
                    pool.tensor_copy(before[:, 0, :], chosen[:, :]).then_inc(s("f_before0"), 1)
                    pool.tensor_tensor(before[:, 1, :], chosen[:, :], both[:, 0, :], ALU.add).then_inc(s("f_before"), 1)
                    ge(pool, "f_before", j + 1)
                    ge(pool, "f_before0", j + 1)
                    pool.tensor_tensor(chosen[:, :], before[:, 1, :], both[:, 1, :], ALU.add).then_inc(s("f_chosen"), 1)
                if on(u - 5):
                    ge(pool, "f_aggr", u - 4)
                    pool.tensor_tensor(vef[:, :], agf[:, 1:2], epsc[:, 0:1], ALU.add).then_inc(s("f_veps"), 1)
                    ge(pool, "f_veps", u - 4)
                    pool.tensor_tensor(norm3[:, bass.ds(u - 5, 1), 1], vef[:, :], mhalf[:, 0:1], ALU.pow)\
                        .then_inc(s("f_rstd"), 1)
                    pool.tensor_copy(norm3[:, bass.ds(u - 5, 1), 0], agf[:, 0:1]).then_inc(s("f_norm"), 1)
                if on(t):
                    rstd(agc, rsc, "c", t)
                if on(u):
                    rstd(agl, rsl, "l", u)
                if on(u - 1):
                    blocks("b", kT, "a", u - 1, parity(par, 1))
                if on(t):
                    blocks("d", xkT, "e", t, p)
                if par == 0 and on2(j):
                    ge(pool, "f_rows", j + 1)
                    ge(pool, "f_slot", j + 1)
                    alone(pool)
                    for b in range(2):
                        for k in range(2):
                            pool.indirect_dma_start(rows_d, bass.IndirectOffsetOnAxis(ap=slot[:, b, k:k + 1], axis=0),
                                                    xrow[:, b, k, :], None).then_inc(s("dispatched"), 16)

            run_bodies(pool, step)

            def tile_out(i, q):
                ge(pool, "y_ready", i * 2 + 2, ANY)
                ge(pool, "x_dest", i + 1, ANY)
                ge(pool, "y_out", i * (16 * TS), ANY)
                alone(pool)
                for sub in range(TS):
                    pool.indirect_dma_start(y_d, bass.IndirectOffsetOnAxis(ap=dest[:, q, sub:sub + 1], axis=0),
                                            y[q][:, sub, :], None, bounds_check=2 * B * L - 1, oob_is_err=False)\
                        .then_inc(s("y_out"), 16)

            run_tiles(pool, tile_out)

        @block.scalar
        def _(act):
            act.wait_ge(s("const_in"), 16 * CONST)
            act.wait_ge(s("pool_const"), 1)

            def exp(k, t, g):
                ge(act, f"{k}_shifted", 4 * t + g + 1, 4 * B)
                act.activation(pr[k][:, :, :], pr[k][:, :, :], ACT.Exp, scale=DH ** -0.5).then_inc(s(f"{k}_probs"), 1)

            def copy_T(k, t, g):
                ge(act, f"{k}_probsT", 4 * t + g + 1, 4 * B)
                ge(act, f"{k}_pv", 4 * t + g, 4 * B)
                act.activation(prT[k][:, :, :], ps_at[:, :].rearrange("p (j l) -> p j l", j=HQ), ACT.Copy)\
                    .then_inc(s(f"{k}_prT"), 1)

            def copy_o(k, t, name):
                ge(act, f"{k}_pv", 4 * t + 4, 4 * B)
                ge(act, f"{name}_oT_turned", t)
                act.activation(oT[k][:, :, :], ps_o[k][:, :].rearrange("p (g l) -> p g l", g=NQ), ACT.Copy)\
                    .then_inc(s(f"{k}_oT"), 1)

            def two(src):
                return src[:, 0:NC * L].rearrange("p (c l) -> p c l", c=NC)

            def step(u, i, par):
                q = quads(u)
                tA, pA, tC, pC, tG = u - 1, parity(par, 1), u - 3, parity(par, 3), u - 5
                j = i - 1
                topk = par == 1 and on2(j)
                jF = (i - 3) if par else (i - 4)
                for m in range(8):
                    if m == 1 and on(tC):
                        copy_o("b", tC, "c")
                    if m == 2 and on(tG):
                        copy_o("d", tG, "g")
                    if m == 0 and on(tA):
                        ge(act, "a_transposed", tA + 1)
                        ge(act, "a_projected", tA)
                        act.activation(xnT[:, :, :], two(m0), ACT.Copy).then_inc(s("a_xnT"), 1)
                    if m == 0 and on(u - 6):
                        ge(act, "f_turned", u - 5)
                        ge(act, "f_gated", (i - 3) if par else (i - 3), B // 2)
                        act.activation(x3p[:, :, par * L:(par + 1) * L], m2[:, 256:512].rearrange("p (c l) -> p c l", c=NC),
                                       ACT.Copy).then_inc(s("f_x3T"), 1)
                    if m == 1 and on(tC):
                        ge(act, "e_transposed", tC + 1)
                        ge(act, "e_projected", tC)
                        act.activation(cT[:, :, :], two(m2), ACT.Copy).then_inc(s("e_cT"), 1)
                    if m == 1 and par == 0 and on2(jF):
                        ge(act, "f_shifted", jF + 1)
                        act.activation(pe_[:, :, :], lg[:, :, :], ACT.Exp).then_inc(s("f_exp"), 1)
                    if m == 2 and on(tA):
                        ge(act, "a_projected", tA + 1)
                        ge(act, "b_scores", 4 * tA - 4, 4 * B)
                        for c in range(NC):
                            last = act.activation(qT["b"][:, pA, c, :], m0[:, c * L:(c + 1) * L], ACT.Identity,
                                                  bias=bq_s[:, c:c + 1])
                        last.then_inc(s("b_queries"), 1)
                    if m == 4 and on(tA):
                        ge(act, "a_ksbd", tA + 1)
                        ge(act, "b_keys", tA)
                        act.activation(kT[:, :, :], two(m0), ACT.Copy).then_inc(s("a_kT"), 1)
                    if m == 5 and on(tC):
                        ge(act, "c_ctx_turned", tC + 1)
                        ge(act, "c_out", tC)
                        ge(act, "a_averaged", tA + 1)
                        act.activation(ctxT[:, :, :], two(m1), ACT.Copy).then_inc(s("c_ctxT"), 1)
                    if m == 5 and on(tA):
                        ge(act, "a_averaged", tA + 1)
                        ge(act, "c_umean", tA - 1)
                        act.activation(mean_v[:, pA, :], m1[:, 256:512], ACT.Copy).then_inc(s("a_mean"), 1)
                    if m == 6 and par == 1 and on2(jF):
                        ge(act, "f_gated", jF + 1)
                        ge(act, "f_back", jF)
                        act.activation(lgT[:, :], m1[0:NE, 0:2 * L], ACT.Identity, bias=gb_s[:, 0:1]).then_inc(s("f_lgT"), 1)
                    if m == 6 and on(tC):
                        ge(act, "e_projected", tC + 1)
                        ge(act, "d_keys", tC)
                        act.activation(xkT[:, :, :], two(m2), ACT.Relu).then_inc(s("e_kT"), 1)
                        ge(act, "d_pv", 4 * tC - 4, 4 * B)
                        act.activation(vh["d"][:, pC, :, 0:DH], m2[:, 256:512].rearrange("p (h d) -> p h d", h=H),
                                       ACT.Relu).then_inc(s("d_values"), 1)
                    if m == 7 and on(tC):
                        ge(act, "c_xn_turned", tC + 1)
                        ge(act, "c_queried", tC)
                        act.activation(xn2T[:, :, :], two(m1), ACT.Copy).then_inc(s("c_xnT"), 1)
                    if on(q[m][1]):
                        exp(*q[m])
                    if on(q[m - 1][1]):
                        copy_T(*q[m - 1])
                    if m == 7 and on(tC):
                        ge(act, "c_queried", tC + 1)
                        ge(act, "d_scores", 4 * tC - 4, 4 * B)
                        act.activation(qT["d"][:, pC, :, :], two(m1), ACT.Relu).then_inc(s("d_queries"), 1)
                    if m == 7 and par == 0 and on2(j):
                        ge(act, "k_turned", j + 1)
                        ge(act, "k_taken", j * 5, 5 * B)
                        act.activation(mT[0][:, :], m2[0:32, 0:L], ACT.Copy).then_inc(s("k_mT"), 1)

            run_bodies(act, step)

            def tile(i, q):
                def turned(i, q):
                    for c in range(NC):
                        ge(act, "x_turned", i * 2 + c + 1, ANY)
                        if c == 0:
                            ge(act, "h1_out", i * 2, ANY)
                        act.activation(x3T[c], bank[6 + c][:, :], ACT.Copy).then_inc(s("x_T"), 1)

                def first(i, q):
                    ge(act, "h1_out", i * 2 + 1, ANY)
                    ge(act, "h2_out", i * 2, ANY)
                    act.activation(h1[:, 0, :], bank[0][:, :], ACT.Relu, bias=wt[:, q, 3 * WL:3 * WL + 1]).then_inc(s("h1_0"), 1)

                if is_int(i) and i == 0:
                    act.wait_ge(s("tile_in0"), 48)
                    turned(0, 0)
                    first(0, 0)
                more = not is_int(i) or i + 1 < NT
                if more:
                    turned(i + 1, (q + 1) % TB)
                ge(act, "h2_out", i * 2 + 1, ANY)
                ge(act, "h3_out", i * 2, ANY)
                act.activation(h2[:, 0, :], bank[2][:, :], ACT.Relu, bias=wt[:, q, 3 * WL + NC:3 * WL + NC + 1])\
                    .then_inc(s("h2_0"), 1)
                if more:
                    first(i + 1, (q + 1) % TB)

            run_tiles(act, tile, 1)

            def group_out(g, q):
                ge(act, "added", g + 1, ANY)
                act.dma_start(out[bass.ds(g * GT, GT), :, :].rearrange("b p n -> p b n"),
                              xall[:, bass.ds(g * GT, GT), :]).then_inc(s("out_done"), 16)

            run_groups(act, group_out)
            act.wait_ge(s("out_done"), 16 * NG)

        @block.vector
        def _(dve):
            dve.wait_ge(s("const_in"), 16 * CONST)
            dve.wait_ge(s("pool_const"), 1)
            dve.tensor_copy(idx_f[:, :], idx_i[:, :]).then_inc(s("idx"), 1)
            dve.wait_ge(s("idx"), 1)
            dve.tensor_scalar(idx_n[:, :], idx_f[:, :], 0.0, float(L), ALU.is_lt, ALU.mult).then_inc(s("idx"), 1)
            dve.wait_ge(s("idx"), 2)
            dve.tensor_tensor(idx_f[:, :], idx_f[:, :], idx_n[:, :], ALU.add).then_inc(s("idx"), 1)
            dve.wait_ge(s("idx"), 3)
            dve.tensor_scalar(idx_n[:, :], idx_f[:, :], 0.0, float(L - 1), ALU.max, ALU.min).then_inc(s("idx"), 1)
            dve.wait_ge(s("idx"), 4)
            dve.tensor_scalar(samp[:, 0:U], idx_n[:, :], kcol[:, 0:1], None, ALU.is_equal).then_inc(s("idx"), 1)
            dve.wait_ge(s("idx"), 5)
            dve.reduce_sum(smax[:, 0:1], samp[:, 0:U], AX).then_inc(s("idx"), 1)
            dve.wait_ge(s("idx"), 6)
            dve.tensor_scalar(samp[:, U:UM], smax[:, 0:1], 1.0 / U, None, ALU.mult)
            dve.tensor_copy(tri[:, :], tri_f[:, :]).then_inc(s("samp_ready"), 1)

            def quad(k, t, g, between):
                S4 = ps_s[k][:, :].rearrange("p (j l) -> p j l", j=HQ)
                ge(dve, f"{k}_scores", 4 * t + g + 1, 4 * B)
                dve.reduce_max(mx[k][:, :], S4, AX).then_inc(s(f"{k}_max"), 1)
                between()
                ge(dve, f"{k}_max", 4 * t + g + 1, 4 * B)
                ge(dve, f"{k}_probsT", 4 * t + g, 4 * B)
                dve.tensor_tensor(pr[k][:, :, :], S4, mx[k][:, :].unsqueeze(2).to_broadcast([128, HQ, L]),
                                  ALU.subtract).then_inc(s(f"{k}_shifted"), 1)

            def top_max(j, r):
                ge(dve, "k_mT", j + 1)
                ge(dve, "k_taken", j * 5 + r, ANY)
                alone(dve)
                dve.max(top8[:, :], mT[r % 2][:, :]).then_inc(s("k_max"), 1)

            def top_taken(j, r):
                ge(dve, "k_max", j * 5 + r + 1, ANY)
                alone(dve)
                dve.match_replace(mT[(r + 1) % 2][:, :], top8[:, :], mT[r % 2][:, :], GONE).then_inc(s("k_taken"), 1)

            def stats(src, stt, ag, name, t):
                alone(dve)
                dve.bn_stats(stt[:, :], src).then_inc(s(f"{name}_stats"), 1)
                ge(dve, f"{name}_stats", t + 1)
                alone(dve)
                dve.bn_aggr(ag[:, :], stt[:, :]).then_inc(s(f"{name}_aggr"), 1)

            def tile(t):
                return xall[:, bass.ds(t, 1), :].rearrange("p b n -> p (b n)")

            def heads(ap):
                return ap.rearrange("p (h d) -> p h d", h=H)

            def step(u, i, par):
                q = quads(u)
                tA, pA, tC, pC, tG = u - 1, parity(par, 1), u - 3, parity(par, 3), u - 5
                j = i - 1
                topk = par == 1 and on2(j)
                jF = i - 4
                gate = par == 0 and on2(jF)
                for m in range(8):
                    def between():
                        if topk and m == 0:
                            top_max(j, 0)
                        if topk and m == 1:
                            top_taken(j, 1)
                        if topk and m == 2:
                            top_taken(j, 3)

                    if on(q[m][1]):
                        quad(*q[m], between)
                    else:
                        between()
                    if m == 0 and gate:
                        L8 = m1[:, 0:2 * NE].rearrange("p (b e) -> p b e", b=2)
                        ge(dve, "f_back", jF + 1)
                        dve.reduce_max(gm[:, :], L8, AX).then_inc(s("f_gm"), 1)
                        ge(dve, "f_gm", jF + 1)
                        dve.tensor_tensor(lg[:, :, :], L8, gm[:, :].unsqueeze(2).to_broadcast([128, 2, NE]), ALU.subtract)\
                            .then_inc(s("f_shifted"), 1)
                    if m == 2 and gate:
                        ge(dve, "f_exp", jF + 1)
                        dve.reduce_sum(gs[:, :], pe_[:, :, :], AX).then_inc(s("f_gsum"), 1)
                        ge(dve, "f_gsum", jF + 1)
                        dve.reciprocal(gr[:, :], gs[:, :]).then_inc(s("f_grec"), 1)
                        ge(dve, "f_grec", jF + 1)
                        dve.tensor_tensor(probs[:, :, :], pe_[:, :, :], gr[:, :].unsqueeze(2).to_broadcast([128, 2, NE]),
                                          ALU.mult).then_inc(s("f_p"), 1)
                        ge(dve, "f_p", jF + 1)
                        dve.tensor_copy(weigh[:, bass.ds(jF * 2, 2), :], probs[:, :, 0:2]).then_inc(s("f_weigh"), 1)
                        alone(dve)
                        for b in range(2):
                            last = dve.max(pt8[:, b, :], probs[:, b, :])
                        last.then_inc(s("f_top"), 1)
                    if m == 3 and gate:
                        ge(dve, "f_top", jF + 1)
                        alone(dve)
                        for b in range(2):
                            last = dve.max_index(pi8[:, b, :], pt8[:, b, :], probs[:, b, :])
                        last.then_inc(s("f_ti"), 1)
                        ge(dve, "f_ti", jF + 1)
                        dve.tensor_copy(pf2[:, :, :], pi8[:, :, 0:2]).then_inc(s("f_tf"), 1)
                        ge(dve, "f_tf", jF + 1)
                        dve.tensor_tensor(oh[:, :, :, :].rearrange("p b k e -> p (b k) e"),
                                          iota8[:, :].unsqueeze(1).to_broadcast([128, 4, NE]),
                                          pf2[:, :, :].rearrange("p b k -> p (b k)").unsqueeze(2).to_broadcast([128, 4, NE]),
                                          ALU.is_equal).then_inc(s("f_oh"), 1)
                        ge(dve, "f_oh", jF + 1)
                        ge(dve, "f_chosen", jF)
                        dve.tensor_tensor(both[:, :, :], oh[:, :, 0, :], oh[:, :, 1, :], ALU.add).then_inc(s("f_both"), 1)
                    if m == 0 and topk:
                        top_taken(j, 0)
                        top_max(j, 1)
                    if m == 1 and topk:
                        top_max(j, 2)
                    if m == 1 and on(tA):
                        ge(dve, "a_kv", tA + 1)
                        ge(dve, "a_sampled", tA)
                        dve.tensor_tensor(ktok[:, :], m0[:, 0:D], bk_s[:, :], ALU.add).then_inc(s("a_ktok"), 1)
                        ge(dve, "b_pv", 4 * tA - 4, 4 * B)
                        dve.tensor_tensor(vh["b"][:, pA, :, 0:DH], heads(m0[:, D:2 * D]), heads(bv_s[:, :]), ALU.add)\
                            .then_inc(s("b_values"), 1)
                    if m == 1 and topk:
                        top_taken(j, 2)
                        top_max(j, 3)
                    if m == 2 and topk:
                        top_max(j, 4)
                        ge(dve, "k_max", j * 5 + 5, ANY)
                        dve.tensor_copy(top2[:, 0:U % 8], top8[:, 0:U % 8]).then_inc(s("k_top2"), 1)
                        ge(dve, "k_top2", j + 1)
                        alone(dve)
                        dve.match_replace(mT[1][:, :], top2[:, :], mT[0][:, :], GONE).then_inc(s("k_taken"), 1)
                        ge(dve, "k_taken", j * 5 + 5, ANY)
                        ge(dve, "k_sel_turned", j)
                        dve.tensor_scalar(selT[:, :], mT[1][:, :], GONE, None, ALU.is_equal).then_inc(s("k_selT"), 1)
                    if m == 3 and topk:
                        ge(dve, "k_sel_turned", j + 1)
                        ge(dve, "c_umean", 2 * j)
                        dve.tensor_copy(sel[:, :, :], m2[:, 0:32].rearrange("p (b h) -> p b h", b=2)).then_inc(s("k_sel1"), 1)
                        dve.tensor_scalar(nsel[:, :, :], m2[:, 0:32].rearrange("p (b h) -> p b h", b=2), -1.0, 1.0,
                                          ALU.mult, ALU.add).then_inc(s("k_sel"), 1)
                    if m == (3 if par else 2) and on(tC):
                        jC = (i - 1) if par else (i - 2)
                        O = m1[:, :].rearrange("p (h e) -> p h e", h=H)
                        ge(dve, "c_oT_turned", tC + 1)
                        dve.reciprocal(rden[:, :], O[:, :, DH]).then_inc(s("c_rden"), 1)
                        ge(dve, "c_rden", tC + 1)
                        ge(dve, "k_sel", jC + 1)
                        dve.tensor_tensor(wsel[:, :], rden[:, :], sel[:, pC, :], ALU.mult).then_inc(s("c_wsel"), 1)
                        ge(dve, "c_wsel", tC + 1)
                        dve.tensor_tensor(heads(ctxa[:, :]), O[:, :, 0:DH],
                                          wsel[:, :].unsqueeze(2).to_broadcast([128, H, DH]), ALU.mult)\
                            .then_inc(s("c_scaled"), 1)
                        ge(dve, "c_scaled", tC + 1)
                        ge(dve, "c_umean", tC + 1)
                        ge(dve, "c_ctx_turned", tC)
                        dve.tensor_tensor(ctxv[:, :], ctxa[:, :], umean[:, :], ALU.add).then_inc(s("c_context"), 1)
                    if m == 3 and on(tA):
                        ge(dve, "a_sampled", tA + 1)
                        ge(dve, "a_scored", 2 * tA, 2 * B)
                        dve.tensor_tensor(ksbd[:, :, :, :],
                                          m0[:, 256:256 + NC * UM].rearrange("p (c u) -> p c u", c=NC).unsqueeze(2)
                                          .to_broadcast([128, NC, HQ, UM]),
                                          hmask[:, :].unsqueeze(1).unsqueeze(3).to_broadcast([128, NC, HQ, UM]),
                                          ALU.mult).then_inc(s("a_ksbd"), 1)
                    if m == 4 and on(tG):
                        O = m2[:, :].rearrange("p (h e) -> p h e", h=H)
                        ge(dve, "g_oT_turned", tG + 1)
                        dve.reciprocal(xrden[:, :], O[:, :, DH]).then_inc(s("g_rden"), 1)
                        ge(dve, "g_rden", tG + 1)
                        dve.tensor_tensor(heads(xatt[:, :]), O[:, :, 0:DH],
                                          xrden[:, :].unsqueeze(2).to_broadcast([128, H, DH]), ALU.mult)\
                            .then_inc(s("g_scaled"), 1)
                        ge(dve, "g_scaled", tG + 1)
                        dve.tensor_tensor(tile(tG), xatt[:, :], tile(tG), ALU.add).then_inc(s("g_x2"), 1)
                    if m == 4 and on(tG):
                        ge(dve, "g_x2", tG + 1)
                        ge(dve, "f_norm", tG)
                        ge(dve, "f_veps", tG)
                        stats(tile(tG), stf, agf, "f", tG)
                    if m in (5, 6) and on(tA):
                        r = m - 5
                        ge(dve, "a_scored", 2 * tA + r + 1, 2 * B)
                        W4 = smax[:, :].rearrange("p (c r j) -> p c r j", c=NC, r=2)
                        V4 = mtok[:, pA, :].rearrange("p (c r j) -> p c r j", c=NC, r=2)
                        SS = m0[:, 0:NC * HQ * UM].rearrange("p (c j u) -> p c j u", c=NC, j=HQ)
                        dve.reduce_max(W4[:, :, r, :], SS[:, :, :, 0:U], AX).then_inc(s("a_smax"), 1)
                        ge(dve, "a_smax", tA * 2 + r + 1, 2 * B)
                        ge(dve, "k_turned", i if par else i - 1, B // 2)
                        dve.tensor_tensor(V4[:, :, r, :], W4[:, :, r, :], SS[:, :, :, U], ALU.subtract)\
                            .then_inc(s("a_m"), 1)
                    if m == 5 and on(tC):
                        ge(dve, "c_out", tC + 1)
                        ge(dve, "c_xb", tC + 1)
                        dve.tensor_tensor(tile(tC), m1[:, 0:D], tile(tC), ALU.add).then_inc(s("c_x1"), 1)
                        ge(dve, "c_x1", tC + 1)
                        stats(tile(tC), stc, agc, "c", tC)
                    if m == 6 and gate:
                        ge(dve, "f_pos", jF + 1)
                        dve.tensor_tensor(posE[:, :, :], m1[:, 0:2 * NE].rearrange("p (b e) -> p b e", b=2),
                                          row0[:, :].unsqueeze(1).to_broadcast([128, 2, NE]), ALU.add).then_inc(s("f_posE"), 1)
                    if m == 6 and on(tC):
                        ge(dve, "c_rstd", tC + 1)
                        ge(dve, "c_aggr", tC + 1)
                        ge(dve, "c_xn_turned", tC)
                        dve.tensor_scalar(xn2[:, :], tile(tC), agc[:, 0:1], rsc[:, 1:2], ALU.subtract, ALU.mult)\
                            .then_inc(s("c_xn"), 1)
                    if m == 0 and on(u):
                        ge(dve, f"x_in{par}", i * 16 + 16, 16 * B)
                        ge(dve, "l_rstd", u)
                        stats(tile(u), stl, agl, "l", u)
                    if m == 6 and on(u):
                        ge(dve, "l_rstd", u + 1)
                        ge(dve, "l_aggr", u + 1)
                        ge(dve, "a_transposed", u - 1)
                        dve.tensor_scalar(xn[:, par, :], tile(u), agl[:, 0:1], rsl[:, 1:2], ALU.subtract, ALU.mult)\
                            .then_inc(s("l_xn"), 1)
                    if m == 6 and gate:
                        ge(dve, "f_posE", jF + 1)
                        for b in range(2):
                            last = dve.tensor_tensor(ohp[:, b, :, :], oh[:, b, :, :],
                                                     posE[:, b:b + 1, :].to_broadcast([128, 2, NE]), ALU.mult)
                        last.then_inc(s("f_ohp"), 1)
                        ge(dve, "f_ohp", jF + 1)
                        dve.reduce_sum(slot_f[:, :, :].rearrange("p b k -> p (b k)"),
                                       ohp[:, :, :, :].rearrange("p b k e -> p (b k) e"), AX).then_inc(s("f_slotf"), 1)
                        ge(dve, "f_slotf", jF + 1)
                        ge(dve, "dispatched", jF * 64, ANY)
                        dve.tensor_copy(slot[:, :, :], slot_f[:, :, :]).then_inc(s("f_slot"), 1)
                    if m == 7 and on(tG):
                        ge(dve, "f_norm", tG + 1)
                        ge(dve, "f_rstd", tG + 1)
                        ge(dve, "f_turned", tG - 1)
                        dve.tensor_scalar(xn3[:, parity(par, 5), :], tile(tG), norm3[:, bass.ds(tG, 1), 0],
                                          norm3[:, bass.ds(tG, 1), 1], ALU.subtract, ALU.mult).then_inc(s("f_xn"), 1)
                    if m == 7 and gate:
                        ge(dve, "f_norm", jF * 2 + 2)
                        ge(dve, "f_rstd", jF * 2 + 2)
                        for b in range(2):
                            for k in range(2):
                                dve.tensor_scalar(xrow[:, b, k, 0:D], tile(jF * 2 + b),
                                                  norm3[:, bass.ds(jF * 2 + b, 1), 0], norm3[:, bass.ds(jF * 2 + b, 1), 1],
                                                  ALU.subtract, ALU.mult)
                        dve.tensor_copy(xrow[:, :, :, D], token[:, bass.ds(jF * 2, 2), :]).then_inc(s("f_rows"), 1)

            run_bodies(dve, step)

            def link(ins):
                links[0] += 1
                ins.then_inc(s("t_link"), 1)
                dve.wait_ge(s("t_link"), links[0])

            links = [0]
            dve.wait_ge(s("t_counted"), 1)
            link(dve.tensor_copy(cnt[:, :], m1[:, 0:NE]))
            link(dve.tensor_tensor(cmpS[:, :, :], cnt[:, :].unsqueeze(2).to_broadcast([128, NE, B * L // TR]),
                                   steps_c[:, :].unsqueeze(1).to_broadcast([128, NE, B * L // TR]), ALU.is_gt))
            link(dve.reduce_sum(nt[:, :], cmpS[:, :, :], AX))
            link(dve.tensor_tensor(ntm[:, :, :], upto[:, :, :], nt[:, :].unsqueeze(1).to_broadcast([128, NE, NE]), ALU.mult))
            link(dve.reduce_sum(cum[:, :], ntm[:, :, :], AX))
            link(dve.tensor_scalar(last1[:, :], cum[:, NE - 1:NE], -1.0, None, ALU.add))
            link(dve.tensor_scalar(ti[:, :], tile_c[:, :], last1[:, 0:1], None, ALU.min))
            link(dve.tensor_tensor(cmpT[:, :, :], ti[:, :].unsqueeze(2).to_broadcast([128, NT, NE]),
                                   cum[:, :].unsqueeze(1).to_broadcast([128, NT, NE]), ALU.is_ge))
            link(dve.reduce_sum(te[:, :], cmpT[:, :, :], AX))
            link(dve.tensor_tensor(cmpN[:, :, :], cmpT[:, :, :], nt[:, :].unsqueeze(1).to_broadcast([128, NT, NE]), ALU.mult))
            link(dve.reduce_sum(tn[:, :], cmpN[:, :, :], AX))
            link(dve.tensor_tensor(tn[:, :], ti[:, :], tn[:, :], ALU.subtract))
            link(dve.tensor_scalar(tn[:, :], tn[:, :], float(TR), None, ALU.mult))
            link(dve.tensor_scalar(trow[:, :], te[:, :], float(RC), None, ALU.mult))
            link(dve.tensor_tensor(trow[:, :], trow[:, :], tn[:, :], ALU.add))
            link(dve.tensor_tensor(pad0[:, :], cnt[:, :], row0[:, :], ALU.add))
            link(dve.tensor_copy(te_i[:, :], te[:, :]))
            link(dve.tensor_copy(trow_i[:, :], trow[:, :]))
            dve.tensor_copy(pad_i[:, :], pad0[:, :]).then_inc(s("t_table"), 1)

            def tile_of_expert(i, q):
                def first(i, q):
                    dve.wait_ge(s(f"tile_in{q}"), tiles_in(i, q))
                    ge(dve, "y_out", (i - TB + 1) * (16 * TS), ANY)
                    dve.tensor_copy(dest[:, q, :], xs[:, q, :, D]).then_inc(s("x_dest"), 1)
                    ge(dve, "h1_out", i * 2 + 2, ANY)
                    ge(dve, "h2_out", i * 2, ANY)
                    dve.tensor_scalar(h1[:, 1, :], bank[1][:, :], wt[:, q, 3 * WL + 1:3 * WL + 2], 0.0, ALU.add, ALU.max)\
                        .then_inc(s("h1_1"), 1)

                if is_int(i) and i == 0:
                    first(0, 0)
                ge(dve, "h2_out", i * 2 + 2, ANY)
                ge(dve, "h3_out", i * 2, ANY)
                dve.tensor_scalar(h2[:, 1, :], bank[3][:, :], wt[:, q, 3 * WL + NC + 1:3 * WL + NC + 2], 0.0, ALU.add, ALU.max)\
                    .then_inc(s("h2_1"), 1)
                if not is_int(i) or i + 1 < NT:
                    first(i + 1, (q + 1) % TB)
                for hf in range(2):
                    ge(dve, "h3_out", i * 2 + hf + 1, ANY)
                    ge(dve, "y_out", (i - TB + 1) * (16 * TS), ANY)
                    dve.tensor_tensor(y[q][:, 2 * hf:2 * hf + 2, :], bank[4 + hf][:, :].rearrange("p (t n) -> p t n", t=2),
                                      b3r[:, q:q + 1, :].to_broadcast([128, 2, D]), ALU.add).then_inc(s("y_ready"), 1)

            run_tiles(dve, tile_of_expert, 1)

            def add_results(g, q):
                dve.wait_ge(s(f"results_in{q}"), results(g, q))
                for k in range(2):
                    for t in range(GT):
                        a = tile(g * GT + t)
                        last = dve.scalar_tensor_tensor(a, yt[q][:, k, t, :], weigh[:, bass.ds(g * GT + t, 1), k], a,
                                                        ALU.mult, ALU.add)
                    if k == 0:
                        last.then_inc(s("added0"), 1)
                        ge(dve, "added0", g + 1, ANY)
                last.then_inc(s("added"), 1)

            run_groups(dve, add_results)

        @block.tensor
        def _(pe):
            mm = nc.tensor.matmul

            def scores(k, t, g, p):
                c, r = g // 2, g % 2
                rows = slice(64 * r, 64 * r + 64)
                if g == 0:
                    ge(pe, f"{k}_queries", t + 1)
                    ge(pe, f"{k}_keys", t + 1)
                ge(pe, f"{k}_shifted", 4 * t + g, 4 * B)
                mm(ps_s[k][:, :], qT[k][rows, p, c, :], kbd[k][rows, p, c, :, :].rearrange("p j l -> p (j l)"),
                   start=True, stop=True).then_inc(s(f"{k}_scores"), 1)

            def turn_probs(k, t, g, u):
                ge(pe, f"{k}_probs", 4 * t + g + 1, 4 * B)
                if k == "b":
                    ge(pe, "d_prT", 4 * (u - 4) + g, 4 * B)
                    if is_int(t):
                        ge(pe, "b_prT", 4 * t + g, 4 * B)
                else:
                    ge(pe, "b_prT", 4 * (u - 2) + g + 1 if g < 3 else 4 * (u - 3) + 4, 4 * B)
                    if is_int(t):
                        ge(pe, "d_prT", 4 * t + g, 4 * B)
                for j in range(HQ):
                    last = nc.tensor.transpose(ps_at[:, j * L:(j + 1) * L], pr[k][:, j, :], ident[:, :])
                last.then_inc(s(f"{k}_probsT"), 1)

            def pv(k, t, g, p):
                ge(pe, f"{k}_prT", 4 * t + g + 1, 4 * B)
                if g == 0:
                    ge(pe, f"{k}_values", t + 1)
                    ge(pe, f"{k}_oT", t)
                for j in range(HQ):
                    last = mm(ps_o[k][HS * j:HS * j + HS, g * L:(g + 1) * L], vh[k][:, p, HQ * g + j, :], prT[k][:, j, :],
                              start=True, stop=True, skip_group_check=True)
                last.then_inc(s(f"{k}_pv"), 1)

            def turn(dst, src, n=NC):
                for c in range(n):
                    last = nc.tensor.transpose(dst[:, c * L:(c + 1) * L], src[:, c * 128:(c + 1) * 128], ident[:, :])
                return last

            def rows_out(dst, w, src):
                for c in range(NC):
                    for k in range(NC):
                        last = mm(dst[:, c * L:(c + 1) * L], w[:, k, c * 128:(c + 1) * 128], src[:, k, :],
                                  start=(k == 0), stop=(k == NC - 1))
                return last

            pe.wait_ge(s("const_in"), 16 * CONST)
            pe.wait_ge(s("pool_const"), 1)
            pe.wait_ge(s("samp_ready"), 1)

            def step(u, i, par):
                q = quads(u)
                tA, pA, tC, pC, tG = u - 1, parity(par, 1), u - 3, parity(par, 3), u - 5
                j = i - 1
                topk = par == 1 and (not is_int(j) or 0 <= j < B // 2)
                for m in range(8):
                    k, t, g = q[m]
                    if on(t):
                        scores(k, t, g, par)
                    if m == 0 and on(tA):
                        ge(pe, "l_xn", tA + 1)
                        ge(pe, "a_m", 2 * tA, 2 * B)
                        turn(m0, xn[:, pA, :]).then_inc(s("a_transposed"), 1)
                    if m == 0 and on(u - 6):
                        ge(pe, "f_xn", u - 5)
                        ge(pe, "e_kT", tC)
                        ge(pe, "d_values", tC)
                        ge(pe, "g_scaled", tG)
                        if topk:
                            ge(pe, "k_mT", j + 1)
                        turn(m2[:, 256:512], xn3[:, par, :]).then_inc(s("f_turned"), 1)
                    if m == 0 and par == 0 and on2(i - 4):
                        ge(pe, "f_lgT", i - 4 + 1)
                        ge(pe, "d_queries", u - 3)
                        alone(pe)
                        for b in range(2):
                            last = nc.tensor.transpose(m1[:, b * NE:(b + 1) * NE], lgT[:, b * L:(b + 1) * L], ident[0:NE, 0:NE])
                        last.then_inc(s("f_back"), 1)
                    if m == 1 and on(tA):
                        ge(pe, "a_xnT", tA + 1)
                        for k in range(NC):
                            last = mm(m0[:, :], xnT[:, k, :], wkv_s[:, k, :], start=(k == 0), stop=(k == NC - 1))
                        last.then_inc(s("a_kv"), 1)
                    if m == 1 and on(tC):
                        jC = (i - 1) if par else (i - 2)
                        ge(pe, f"ctx_in{pC}", jC * 16 + 16, 16 * B)
                        ge(pe, "e_kT", tC)
                        ge(pe, "d_values", tC)
                        ge(pe, "f_x3T", u - 5)
                        if topk:
                            ge(pe, "k_mT", j + 1)
                        turn(m2, cin[:, pC, :]).then_inc(s("e_transposed"), 1)
                    if m == 1 and on(tC):
                        ge(pe, "b_oT", tC + 1)
                        ge(pe, "d_queries", tC)
                        if par == 0 and on2(i - 4):
                            ge(pe, "f_shifted", i - 4 + 1)
                        turn(m1, oT["b"][:, :, :].rearrange("p g l -> p (g l)"), NQ).then_inc(s("c_oT_turned"), 1)
                    if m == 2 and on(tA):
                        ge(pe, "a_ktok", tA + 1)
                        ge(pe, "b_values", tA + 1)
                        rows_out(m0, wq_s, xnT).then_inc(s("a_projected"), 1)
                    if m == 3 and topk:
                        ge(pe, "k_selT", j + 1)
                        ge(pe, "e_cT", tC + 1)
                        alone(pe)
                        nc.tensor.transpose(m2[:, 0:32], selT[:, :], ident[0:32, 0:32]).then_inc(s("k_sel_turned"), 1)
                    if m == 3 and on(tG):
                        ge(pe, "d_oT", tG + 1)
                        ge(pe, "e_cT", tC + 1)
                        if topk:
                            ge(pe, "k_sel", j + 1)
                        turn(m2, oT["d"][:, :, :].rearrange("p g l -> p (g l)"), NQ).then_inc(s("g_oT_turned"), 1)
                    if m == 3 and on(tA):
                        ge(pe, "b_queries", tA + 1)
                        turn(m0, ktok)
                        for c in range(NC):
                            last = mm(m0[:, 256 + c * UM:256 + (c + 1) * UM], ktok[:, c * 128:(c + 1) * 128], samp[:, :],
                                      start=True, stop=True)
                        last.then_inc(s("a_sampled"), 1)
                    if m in (5, 6) and on(tA):
                        r = m - 5
                        if r == 0:
                            ge(pe, "a_kT", tA + 1)
                            ge(pe, "a_ksbd", tA + 1)
                        else:
                            ge(pe, "a_m", 2 * tA + 1, 2 * B)
                        rows = slice(64 * r, 64 * r + 64)
                        for c in range(NC):
                            last = mm(m0[:, c * HQ * UM:(c + 1) * HQ * UM], qT["b"][rows, pA, c, :],
                                      ksbd[rows, c, :, :].rearrange("p j u -> p (j u)"), start=True, stop=True)
                        last.then_inc(s("a_scored"), 1)
                    if m == 5 and on(tC):
                        ge(pe, "c_ctxT", tC + 1)
                        ge(pe, "a_mean", tA + 1)
                        for k in range(NC):
                            last = mm(m1[:, 0:D], ctxT[:, k, :], wo_s[:, k, :], start=(k == 0), stop=(k == NC - 1))
                        last.then_inc(s("c_out"), 1)
                    if m == 6 and par == 1 and on2(i - 3):
                        ge(pe, "f_x3T", i * 2 - 4)
                        ge(pe, "c_x1", tC + 1)
                        for k in range(NC):
                            last = mm(m1[0:NE, 0:2 * L], gw_s[:, k, :], x3p[:, k, :], start=(k == 0), stop=(k == NC - 1))
                        last.then_inc(s("f_gated"), 1)
                    if m == 6 and par == 0 and on2(i - 4):
                        ge(pe, "f_both", i - 4 + 1)
                        ge(pe, "f_before", i - 4 + 1)
                        ge(pe, "f_before0", i - 4 + 1)
                        ge(pe, "c_x1", tC + 1)
                        P8 = m1[:, 0:2 * NE]
                        mm(P8, ones[:, :], before[:, :, :].rearrange("p b e -> p (b e)"), start=True, stop=False)
                        mm(P8, tri[:, :], both[:, :, :].rearrange("p b e -> p (b e)"), start=False, stop=True)\
                            .then_inc(s("f_pos"), 1)
                    if m == 6 and on(tC):
                        ge(pe, "g_scaled", tG + 1)
                        ge(pe, "e_cT", tC + 1)
                        if topk:
                            ge(pe, "k_sel", j + 1)
                        rows_out(m2, xwk_s, cT)
                        for k in range(NC):
                            last = mm(m2[:, 256:512], cT[:, k, :], xwv_s[:, k, :], start=(k == 0), stop=(k == NC - 1))
                        last.then_inc(s("e_projected"), 1)
                    if m == 7 and on(tC):
                        ge(pe, "c_xn", tC + 1)
                        if par == 1 and on2(i - 3):
                            ge(pe, "f_lgT", i - 3 + 1)
                        if par == 0 and on2(i - 4):
                            ge(pe, "f_posE", i - 4 + 1)
                        turn(m1, xn2).then_inc(s("c_xn_turned"), 1)
                    for back in (2, 1):
                        k, t, g = q[m - back]
                        if on(t) and back == 2:
                            pv(k, t, g, par if m >= 2 else 1 - par)
                        if on(t) and back == 1:
                            turn_probs(k, t, g, u)
                    if m == 4 and on(tC):
                        ge(pe, "c_context", tC + 1)
                        turn(m1, ctxv).then_inc(s("c_ctx_turned"), 1)
                    if m == 4 and on(tA):
                        ge(pe, "a_mean", tA)
                        ge(pe, "b_values", tA + 1)
                        mm(m1[:, 256:512].rearrange("p (h d) -> p h d", h=H), mean_w[:, :], vh["b"][:, pA, :, 0:DH],
                           start=True, stop=True).then_inc(s("a_averaged"), 1)
                    if m == 7 and on(tC):
                        ge(pe, "c_xnT", tC + 1)
                        rows_out(m1, xwq_s, xn2T).then_inc(s("c_queried"), 1)
                    if m == 7 and par == 0 and on2(j):
                        ge(pe, "a_m", j * 4 + 4, 2 * B)
                        ge(pe, "e_kT", tC + 1)
                        ge(pe, "d_values", tC + 1)
                        ge(pe, "g_scaled", tG + 1)
                        nc.tensor.transpose(m2[0:32, 0:L], mtok[:, :, :].rearrange("p b h -> p (b h)"), ident[:, :])\
                            .then_inc(s("k_turned"), 1)

            run_bodies(pe, step)

            pe.wait_ge(s("f_chosen"), B // 2)
            pe.wait_ge(s("f_posE"), B // 2)
            pe.wait_ge(s("d_queries"), B)
            mm(m1[:, 0:NE], ones[:, :], chosen[:, :], start=True, stop=True).then_inc(s("t_counted"), 1)

            def weights(q, layer):
                return wt[:, q, layer * WL:(layer + 1) * WL].rearrange("p (k n) -> p k n", k=NC)

            def turn_rows(i, q):
                pe.wait_ge(s(f"tile_in{q}"), tiles_in(i, q))
                for c in range(NC):
                    ge(pe, "x_T", i * 2 + c - 1, ANY)
                    for sub in range(TS):
                        last = nc.tensor.transpose(bank[6 + c][:, sub * 128:(sub + 1) * 128],
                                                   xs[:, q, sub, c * 128:(c + 1) * 128], ident[:, :])
                    last.then_inc(s("x_turned"), 1)

            def layer1(i, q):
                ge(pe, "x_T", i * 2 + 2, ANY)
                for c in range(NC):
                    ge(pe, f"h1_{c}", i, ANY)
                    for k in range(NC):
                        last = mm(bank[c][:, :], weights(q, 0)[:, k, c * 128:(c + 1) * 128], x3T[k],
                                  start=(k == 0), stop=(k == NC - 1))
                    last.then_inc(s("h1_out"), 1)

            def tile(i, q):
                if is_int(i) and i == 0:
                    turn_rows(0, 0)
                    layer1(0, 0)
                more = not is_int(i) or i + 1 < NT
                if more:
                    turn_rows(i + 1, (q + 1) % TB)
                ge(pe, "h1_0", i + 1, ANY)
                ge(pe, "h1_1", i + 1, ANY)
                for c in range(NC):
                    ge(pe, f"h2_{c}", i, ANY)
                    for k in range(NC):
                        last = mm(bank[2 + c][:, :], weights(q, 1)[:, k, c * 128:(c + 1) * 128], h1[:, k, :],
                                  start=(k == 0), stop=(k == NC - 1))
                    last.then_inc(s("h2_out"), 1)
                if more:
                    layer1(i + 1, (q + 1) % TB)
                ge(pe, "h2_0", i + 1, ANY)
                ge(pe, "h2_1", i + 1, ANY)
                for hf in range(2):
                    ge(pe, "y_ready", i * 2 + hf - 1, ANY)
                    for t in range(2):
                        for k in range(NC):
                            rows = slice((2 * hf + t) * 128, (2 * hf + t + 1) * 128)
                            last = mm(bank[4 + hf][:, t * D:(t + 1) * D], h2[:, k, rows], weights(q, 2)[:, k, :],
                                      start=(k == 0), stop=(k == NC - 1))
                    last.then_inc(s("h3_out"), 1)

            run_tiles(pe, tile, 1)


_OUT = ((B, L, D), "float32")


def kernel(**inputs):
    import numpy as np
    import concourse.bacc as bacc
    from concourse import mybir as mb
    from concourse.bass_utils import run_bass_kernel_spmd

    a = {k: np.ascontiguousarray(v) for k, v in inputs.items()}
    p = "L0_attn_"
    f = "L0_ffn_"
    data = {"x": a["x"], "ctx": a["ctx_1024"], "wq": a[p + "W_q"], "bq": a[p + "b_q"], "wk": a[p + "W_k"],
            "bk": a[p + "b_k"], "wv": a[p + "W_v"], "bv": a[p + "b_v"], "wo": a[p + "W_o"], "bo": a[p + "b_o"],
            "sidx": a[p + "k_sample_idx"],
            "xwqT": np.ascontiguousarray(a["L0_xattn_Wq"].T), "xwkT": np.ascontiguousarray(a["L0_xattn_Wk"].T),
            "xwvT": np.ascontiguousarray(a["L0_xattn_Wv"].T),
            "gwT": np.ascontiguousarray(a[f + "gate_w"].T), "gb": a[f + "gate_b"],
            "experts": np.concatenate(
                [a[f + w].reshape(NE, NC, 128, D).transpose(0, 2, 1, 3).reshape(NE, 128, WL) for w in ("w1", "w2", "w3")]
                + [a[f + b].reshape(NE, NC, 128).transpose(0, 2, 1) for b in ("b1", "b2")], axis=2),
            "b3": a[f + "b3"],
            "ident_d": np.eye(128, dtype=np.float32),
            "hmask_d": (np.arange(128)[:, None] % 64 // 16 == np.arange(4)[None, :]).astype(np.float32),
            "iota8_d": np.tile(np.arange(8, dtype=np.float32), (128, 1)),
            "kcol_d": np.arange(128, dtype=np.float32)[:, None],
            "tri_d": np.triu(np.ones((128, 128), np.float32), 1),
            "token_d": (np.arange(128)[:, None, None] + 128 * np.arange(B)[None, :, None]
                        + B * L * np.arange(2)[None, None, :]).astype(np.float32),
            "row0_d": np.tile(RC * np.arange(NE, dtype=np.float32), (128, 1)),
            "steps_d": np.tile(TR * np.arange(B * L // TR, dtype=np.float32), (128, 1)),
            "upto_d": np.tile(np.tril(np.ones((NE, NE), np.float32)), (128, 1, 1)),
            "tiles_d": np.tile(np.arange(NT, dtype=np.float32), (128, 1))}
    nc = bacc.Bacc("TRN2", target_bir_lowering=False, num_devices=1)
    arrays, args = {}, []
    for name, v in data.items():
        arrays[f"in_{name}"] = v
        args.append(nc.dram_tensor(f"in_{name}", v.shape, mb.dt.from_np(v.dtype), kind="ExternalInput").ap())
    args.append(nc.dram_tensor("out_0", _OUT[0], mb.dt.float32, kind="ExternalOutput").ap())
    decoder_block(nc, *args)
    r = run_bass_kernel_spmd(nc, [arrays], core_ids=[0])
    return r.results[0]["out_0"]
```

```python
import concourse.bass as bass
from concourse import mybir
from contextlib import ExitStack

B, L, D, H, U, NE = 64, 128, 256, 16, 34, 8
DH = D // H
NC = D // 128
HQ = 4
NQ = H // HQ
UM = U + 1
HS = 32
TS = 3
TR = TS * 128
NT = (B * L * 2 + NE * (TR - 1)) // TR
RC = B * L + TR
SL = -(-B * L // TR)
RW = D + 2
NOWHERE = float(4 * B * L)
WL = NC * D
WP = 3 * WL + 2 * NC
TB = 3
EPS = 1e-5
GONE = -3.0e38


def decoder_block(nc, x, ctx, wq, bq, wk, bk, wv, bv, wo, bo, sidx, xwqT, xwkT, xwvT,
                  gwT, gb, experts, b3, ident_d, hmask_d, iota8_d, kcol_d, tri_d, token_d, row0_d,
                  steps_d, upto_d, tiles_d, out):
    f32, i32, u32 = mybir.dt.float32, mybir.dt.int32, mybir.dt.uint32
    bf16 = mybir.dt.bfloat16
    ALU, ACT, AX = mybir.AluOpType, mybir.ActivationFunctionType, mybir.AxisListType.X

    st = ExitStack()
    with st:
        def sb(name, shape, dt=f32):
            return st.enter_context(nc.sbuf_tensor(name, shape, dt))

        def sem(name):
            return st.enter_context(nc.semaphore(name))

        bank = [st.enter_context(nc.psum_tensor(f"bank{i}", [128, 512], f32)) for i in range(8)]
        ps_s = {"b": bank[0], "d": bank[1]}
        ps_at = bank[2]
        ps_o = {"b": bank[3], "d": bank[4]}
        m0, m1, m2 = bank[5], bank[6], bank[7]

        ident = sb("ident", [128, 128])
        hmask = sb("hmask", [128, HQ])
        iota8 = sb("iota8", [128, NE])
        kcol = sb("kcol", [128, 1])
        mean_w = sb("mean_w", [128, 128])
        epsc = sb("epsc", [128, 1])
        mhalf = sb("mhalf", [128, 1])
        wq_s, wo_s = sb("wq_s", [128, NC, D]), sb("wo_s", [128, NC, D])
        wkv_s = sb("wkv_s", [128, NC, 2 * D])
        xwq_s, xwk_s, xwv_s = (sb(n, [128, NC, D]) for n in ("xwq_s", "xwk_s", "xwv_s"))
        bq_s = sb("bq_s", [128, NC])
        bk_s, bv_s, bo_s = (sb(n, [128, D]) for n in ("bk_s", "bv_s", "bo_s"))
        idx_i, idx_f, idx_n = sb("idx_i", [128, U], i32), sb("idx_f", [128, U]), sb("idx_n", [128, U])
        samp = sb("samp", [128, UM])
        gw_s, gb_s = sb("gw_s", [128, NC, NE]), sb("gb_s", [NE, 1])
        tri_f, tri = sb("tri_f", [128, 128]), sb("tri", [128, 128], bf16)
        ones = sb("ones", [128, 128], bf16)
        token = sb("token", [128, B])
        row0 = sb("row0", [128, NE])
        steps_c = sb("steps_c", [128, SL])
        upto = sb("upto", [128, NE, NE])
        tile_c = sb("tile_c", [128, NT])

        xall = sb("xall", [128, B, D])

        xn = sb("xn", [128, 2, D])
        xnT = sb("xnT", [128, NC, L])
        ktok = sb("ktok", [128, D])
        kT = sb("kT", [128, NC, L])
        qT = {"b": sb("qT", [128, 2, NC, L]), "d": sb("xqT", [128, 2, NC, L])}
        kbd = {"b": sb("kbd", [128, 2, NC, HQ, L]), "d": sb("xkbd", [128, 2, NC, HQ, L])}
        vh = {"b": sb("vh", [128, 2, H, HS]), "d": sb("xvh", [128, 2, H, HS])}
        mean_v = sb("mean_v", [128, 2, D])
        ksbd = sb("ksbd", [128, NC, HQ, UM])
        smax = sb("smax", [128, H])
        mtok = sb("mtok", [128, 2, H])
        mT = [sb("mT0", [32, L]), sb("mT1", [32, L])]
        top8 = sb("top8", [32, 8])
        top2 = sb("top2", [32, 8])
        selT = sb("selT", [32, L])
        sel, nsel = sb("sel", [128, 2, H]), sb("nsel", [128, 2, H])
        mx = {"b": sb("mx", [128, HQ]), "d": sb("xmx", [128, HQ])}
        pr = {"b": sb("pr", [128, 2, HQ, L]), "d": sb("xpr", [128, 2, HQ, L])}
        prT = {"b": sb("prT", [128, HQ, L]), "d": sb("xprT", [128, HQ, L])}
        oT = {"b": sb("oT", [128, NQ, L]), "d": sb("xoT", [128, NQ, L])}
        rden, wsel = sb("rden", [128, H]), sb("wsel", [128, H])
        xrden = sb("xrden", [128, H])
        ctxa, ctxv, umean = sb("ctxa", [128, D]), sb("ctxv", [128, D]), sb("umean", [128, D])
        ctxT = sb("ctxT", [128, NC, L])
        xn2, xn2T = sb("xn2", [128, D]), sb("xn2T", [128, NC, L])
        xatt = sb("xatt", [128, D])
        cin = sb("cin", [128, 2, D])
        cT, xkT = sb("cT", [128, NC, L]), sb("xkT", [128, NC, L])
        stl, agl, rsl = sb("stl", [128, 6]), sb("agl", [128, 2]), sb("rsl", [128, 2])
        stc, agc, rsc = sb("stc", [128, 6]), sb("agc", [128, 2]), sb("rsc", [128, 2])

        stf, agf, vef = sb("stf", [128, 6]), sb("agf", [128, 2]), sb("vef", [128, 1])
        norm3 = sb("norm3", [128, B, 2])
        xn3, x3p = sb("xn3", [128, 2, D]), sb("x3p", [128, NC, 2 * L])
        lgT = sb("lgT", [NE, 2 * L])
        lg, pe_ = sb("lg", [128, 2, NE]), sb("pe_", [128, 2, NE])
        gm, gs, gr = sb("gm", [128, 2]), sb("gs", [128, 2]), sb("gr", [128, 2])
        probs = sb("probs", [128, 2, NE])
        pt8, pi8 = sb("pt8", [128, 2, 8]), sb("pi8", [128, 2, 8], u32)
        pf2 = sb("pf2", [128, 2, 2])
        oh = sb("oh", [128, 2, 2, NE])
        both = sb("both", [128, 2, NE], bf16)
        before = sb("before", [128, 2, NE], bf16)
        chosen = sb("chosen", [128, NE], bf16)
        posE, ohp = sb("posE", [128, 2, NE]), sb("ohp", [128, 2, 2, NE])
        slot_f, slot = sb("slot_f", [128, 2, 2]), sb("slot", [128, 2, 2], u32)
        xrow = sb("xrow", [128, 2, 2, RW])

        cnt, nt, cum = sb("cnt", [128, NE]), sb("nt", [128, NE]), sb("cum", [128, NE])
        cmpS = sb("cmpS", [128, NE, SL])
        ntm = sb("ntm", [128, NE, NE])
        cmpT, cmpN = sb("cmpT", [128, NT, NE]), sb("cmpN", [128, NT, NE])
        te, tn, trow = sb("te", [128, NT]), sb("tn", [128, NT]), sb("trow", [128, NT])
        te_i, trow_i = sb("te_i", [128, NT], i32), sb("trow_i", [128, NT], i32)
        pad0, pad_i = sb("pad0", [128, NE]), sb("pad_i", [128, NE], i32)
        padrow = sb("padrow", [128, TS, RW])

        def over(at, *shape):
            n = 1
            for d in shape:
                n *= d
            flat = xall[:, :, :].rearrange("p b n -> p (b n)")[:, at:at + n]
            if len(shape) == 2:
                return flat.rearrange("p (a n) -> p a n", a=shape[0])
            return flat.rearrange("p (a b n) -> p a b n", a=shape[0], b=shape[1])

        wt, b3r = over(0, TB, WP), over(TB * WP, TB, D)
        xs = over(TB * (WP + D), TB, TS, RW)
        y = over(TB * (WP + D + TS * RW), TB, TS, D)
        x3T = [prT[k][:, :, :].rearrange("p j l -> p (j l)")[:, 0:TR] for k in "bd"]
        h1, h2 = (vh[k][:, :, :, :].rearrange("p c h e -> p c (h e)")[:, :, 0:TR] for k in "bd")
        dest = sb("dest", [128, TB, TS], u32)
        rows_d = nc.dram_tensor("dispatched", (NE * RC + TR, RW), f32, kind="Internal").ap()

        S = {}

        def s(name):
            if name not in S:
                S[name] = sem(name)
            return S[name]

        block = st.enter_context(nc.Block())

        STEPS = B + 8
        PRO, LAST = 5, B // 2
        BODIES = (STEPS + 1) // 2

        ANY = 1 << 20

        def is_int(v):
            return isinstance(v, int)

        def on(t):
            return not is_int(t) or 0 <= t < B

        def on2(j):
            return not is_int(j) or 0 <= j < B // 2

        def ge(eng, name, v, most=B):
            if is_int(v):
                v = min(v, most)
                if v <= 0:
                    return
            eng.wait_ge(s(name), v)

        def alone(eng):
            eng.sem_inc(s("passed"), 1)

        def run_bodies(eng, step):
            for i in range(PRO):
                for par in range(2):
                    step(2 * i + par, i, par)
            with eng.Fori(PRO, LAST) as i:
                for par in range(2):
                    step(i * 2 + par, i, par)
            for i in range(LAST, BODIES):
                for par in range(2):
                    step(2 * i + par, i, par)

        def tiles_in(i, q):
            return (i - q + TB) * 16

        HALVES = [range(0, (TS + 1) // 2), range((TS + 1) // 2, TS)]

        def run_tiles(eng, body, ahead=0):
            end = (NT - ahead) // TB * TB
            for i in range(2 * TB):
                body(i, i % TB)
            with eng.Fori(2 * TB, end - TB + 1, TB) as i:
                for q in range(TB):
                    body(i + q, q)
            for i in range(end, NT):
                body(i, i % TB)

        def quads(u):
            return {-3: ("d", u - 5, 2), -2: ("b", u - 3, 3), -1: ("d", u - 5, 3),
                    **{2 * g: ("b", u - 2, g) for g in range(NQ)},
                    **{2 * g + 1: ("d", u - 4, g) for g in range(NQ)}}

        def parity(par, back):
            return (par + back) % 2

        @block.sync
        def _(sp):
            for dst, src in ((ident[:, :], ident_d), (hmask[:, :], hmask_d), (kcol[:, :], kcol_d), (tri_f[:, :], tri_d)):
                sp.dma_start(dst, src).then_inc(s("const_in"), 16)

            def late_constants():
                for dst, src in ((wo_s, wo), (xwq_s, xwqT), (xwk_s, xwkT), (xwv_s, xwvT)):
                    sp.dma_start(dst[:, :, :], src.rearrange("(c p) n -> p c n", p=128)).then_inc(s("late_in"), 16)
                with nc.allow_non_contiguous_dma(reason="small vectors, once"):
                    sp.dma_start(gb_s[:, :], gb.rearrange("(n a) -> n a", a=1)).then_inc(s("late_in"), 16)
                    sp.dma_start(gw_s[:, :, :], gwT.rearrange("(c p) n -> p c n", p=128)).then_inc(s("late_in"), 16)
                    sp.dma_start(bo_s[:, :], bo.rearrange("(a n) -> a n", a=1).to_broadcast([128, D])).then_inc(s("late_in"), 16)
                for dst, src in ((iota8[:, :], iota8_d), (token[:, :], token_d), (row0[:, :], row0_d),
                                 (steps_c[:, :], steps_d), (upto[:, :, :], upto_d), (tile_c[:, :], tiles_d)):
                    sp.dma_start(dst, src).then_inc(s("late_in"), 16)

            def step(u, i, par):
                if on(u):
                    ge(sp, f"x_in{par}", i * 16, 16 * B)
                    alone(sp)
                    sp.dma_start(xall[:, bass.ds(u, 1), :], x[bass.ds(u, 1), :, :].rearrange("b p n -> p b n"))\
                        .then_inc(s(f"x_in{par}"), 16)
                if is_int(u) and u == 1:
                    late_constants()
                t, j = u - 2, i - 1
                if on(t):
                    ge(sp, f"ctx_in{par}", j * 16, 16 * B)
                    alone(sp)
                    ge(sp, "e_transposed", t - 1)
                    alone(sp)
                    sp.dma_start(cin[:, par, :], ctx[bass.ds(t, 1), :, :].rearrange("b p n -> p (b n)"))\
                        .then_inc(s(f"ctx_in{par}"), 16)

                if on(u - 6):
                    ge(sp, "g_x2", u - 5)
                    alone(sp)
                    sp.dma_start(out[bass.ds(u - 6, 1), :, :].rearrange("b p n -> p b n"),
                                 xall[:, bass.ds(u - 6, 1), :]).then_inc(s("x2_out"), 16)

            run_bodies(sp, step)

            sp.wait_ge(s("pool_const"), 1)
            sp.dma_start(rows_d[NE * RC:NE * RC + TR, :].rearrange("(p s) n -> p s n", s=TS), padrow[:, :, :])\
                .then_inc(s("pads_out"), 16)
            sp.wait_ge(s("t_pads"), 1)
            for e in range(NE):
                row = sp.value_load(pad_i[0:1, e:e + 1], min_val=0, max_val=NE * RC - TR)
                sp.dma_start(rows_d[bass.ds(row, TR), :].rearrange("(p s) n -> p s n", s=TS), padrow[:, :, :])\
                    .then_inc(s("pads_out"), 16)
            def weights_in(i, q):
                e = sp.value_load(te_i[0:1, bass.ds(i, 1)], min_val=0, max_val=NE - 1)
                sp.dma_start(wt[:, q, :], experts[bass.ds(e, 1), :, :].rearrange("e p n -> p (e n)"))\
                    .then_inc(s(f"tile_in{q}"), 16)
                sp.dma_start(b3r[:, q, :], b3[bass.ds(e, 1), :].to_broadcast([128, D])).then_inc(s(f"tile_in{q}"), 16)

            sp.wait_ge(s("t_table"), 1)
            sp.wait_ge(s("x2_out"), 16 * B)
            weights_in(0, 0)
            sp.wait_ge(s("pads_out"), 16 * (NE + 1))
            sp.wait_ge(s("dispatched"), 16 * 2 * B)

            def tile_in(i, q):
                if not is_int(i) or i >= TB:
                    ge(sp, "x_dest", i - TB + 1, ANY)
                    alone(sp)
                    ge(sp, "y_ready", (i - TB) * TS + TS, ANY)
                    alone(sp)
                row = sp.value_load(trow_i[0:1, bass.ds(i, 1)], min_val=0, max_val=NE * RC)
                sp.dma_start(xs[:, q, :, :], rows_d[bass.ds(row, TR), :].rearrange("(p s) n -> p s n", s=TS))\
                    .then_inc(s(f"tile_in{q}"), 16)
                if not (is_int(i) and i == 0):
                    weights_in(i, q)

            run_tiles(sp, tile_in)

            sp.wait_ge(s("y_out"), 16 * TS * NT)

        CONST, LATE = 11, 13

        @block.gpsimd
        def _(pool):
            pool.memset(mean_w[:, :], 1.0 / L)
            pool.memset(epsc[:, :], EPS)
            pool.memset(mhalf[:, :], -0.5)
            for k in "bd":
                pool.memset(vh[k][:, :, :, :], 0.0).then_inc(s("zeroed"), 1)
            pool.wait_ge(s("zeroed"), 2)
            for k in "bd":
                pool.memset(vh[k][:, :, :, DH:DH + 1], 1.0).then_inc(s("ones_set"), 1)
            pool.wait_ge(s("ones_set"), 2)
            pool.memset(ones[:, :], 1.0)
            pool.memset(chosen[:, :], 0.0)
            pool.memset(padrow[:, :, 0:D], 0.0)
            pool.memset(padrow[:, :, D:RW], NOWHERE)
            pool.memset(top2[:, :], GONE).then_inc(s("pool_const"), 1)
            pool.wait_ge(s("pool_const"), 1)

            def rstd(aggr, rs, name, t):
                ge(pool, f"{name}_aggr", t + 1)
                pool.tensor_tensor(rs[:, 0:1], aggr[:, 1:2], epsc[:, 0:1], ALU.add).then_inc(s(f"{name}_veps"), 1)
                ge(pool, f"{name}_veps", t + 1)
                pool.tensor_tensor(rs[:, 1:2], rs[:, 0:1], mhalf[:, 0:1], ALU.pow).then_inc(s(f"{name}_rstd"), 1)

            def blocks(k, src, name, t, p):
                ge(pool, f"{name}_kT", t + 1)
                ge(pool, f"{k}_scores", 4 * t - 4, 4 * B)
                pool.tensor_tensor(kbd[k][:, p, :, :, :],
                                   src[:, :, :].unsqueeze(2).to_broadcast([128, NC, HQ, L]),
                                   hmask[:, :].unsqueeze(1).unsqueeze(3).to_broadcast([128, NC, HQ, L]),
                                   ALU.mult).then_inc(s(f"{k}_keys"), 1)

            pool.wait_ge(s("const_in"), 16 * CONST)

            def step(u, i, par):
                if is_int(u) and u == 3:
                    pool.wait_ge(s("late_in"), 16 * LATE)
                t, p = u - 3, parity(par, 3)
                if on(t):
                    ge(pool, "l_xn", t + 1)
                    pool.tensor_tensor(xall[:, bass.ds(t, 1), :].rearrange("p b n -> p (b n)"),
                                       xall[:, bass.ds(t, 1), :].rearrange("p b n -> p (b n)"),
                                       bo_s[:, :], ALU.add).then_inc(s("c_xb"), 1)
                    j = (i - 1) if par else (i - 2)
                    ge(pool, "k_sel", j + 1)
                    ge(pool, "a_mean", t + 1)
                    ge(pool, "c_context", t)
                    pool.tensor_tensor(umean[:, :].rearrange("p (h d) -> p h d", h=H),
                                       mean_v[:, p, :].rearrange("p (h d) -> p h d", h=H),
                                       nsel[:, p, :].unsqueeze(2).to_broadcast([128, H, DH]),
                                       ALU.mult).then_inc(s("c_umean"), 1)
                j = i - 4
                if par == 0 and on2(j):
                    ge(pool, "f_both", j + 1)
                    ge(pool, "f_pos", j)
                    ge(pool, "f_chosen", j)
                    alone(pool)
                    pool.tensor_copy(before[:, 0, :], chosen[:, :]).then_inc(s("f_before0"), 1)
                    pool.tensor_tensor(before[:, 1, :], chosen[:, :], both[:, 0, :], ALU.add).then_inc(s("f_before"), 1)
                    ge(pool, "f_before", j + 1)
                    ge(pool, "f_before0", j + 1)
                    pool.tensor_tensor(chosen[:, :], before[:, 1, :], both[:, 1, :], ALU.add).then_inc(s("f_chosen"), 1)
                if on(u - 5):
                    ge(pool, "f_aggr", u - 4)
                    pool.tensor_tensor(vef[:, :], agf[:, 1:2], epsc[:, 0:1], ALU.add).then_inc(s("f_veps"), 1)
                    ge(pool, "f_veps", u - 4)
                    pool.tensor_tensor(norm3[:, bass.ds(u - 5, 1), 1], vef[:, :], mhalf[:, 0:1], ALU.pow)\
                        .then_inc(s("f_rstd"), 1)
                    pool.tensor_copy(norm3[:, bass.ds(u - 5, 1), 0], agf[:, 0:1]).then_inc(s("f_norm"), 1)
                if on(t):
                    rstd(agc, rsc, "c", t)
                if on(u):
                    rstd(agl, rsl, "l", u)
                if on(u - 1):
                    blocks("b", kT, "a", u - 1, parity(par, 1))
                if on(t):
                    blocks("d", xkT, "e", t, p)
                if par == 0 and on2(j):
                    ge(pool, "f_rows", j + 1)
                    ge(pool, "f_weigh", j + 1)
                    ge(pool, "f_slot", j + 1)
                    alone(pool)
                    for b in range(2):
                        for k in range(2):
                            pool.indirect_dma_start(rows_d, bass.IndirectOffsetOnAxis(ap=slot[:, b, k:k + 1], axis=0),
                                                    xrow[:, b, k, :], None).then_inc(s("dispatched"), 16)

            run_bodies(pool, step)

            def tile_out(i, q):
                if is_int(i) and i == 0:
                    pool.wait_ge(s("x2_out"), 16 * B)
                ge(pool, "y_ready", i * TS + TS, ANY)
                ge(pool, "x_dest", i + 1, ANY)
                ge(pool, "y_out", i * (16 * TS), ANY)
                alone(pool)
                for sub in range(TS):
                    pool.indirect_dma_start(out.rearrange("b p n -> (b p) n"),
                                            bass.IndirectOffsetOnAxis(ap=dest[:, q, sub:sub + 1], axis=0),
                                            y[:, q, sub, :], None, bounds_check=B * L - 1, oob_is_err=False,
                                            compute_op=ALU.add)\
                        .then_inc(s("y_out"), 16)

            run_tiles(pool, tile_out)

        @block.scalar
        def _(act):
            for dst, src in ((wkv_s[:, :, 0:D], wk), (wkv_s[:, :, D:2 * D], wv), (wq_s[:, :, :], wq)):
                act.dma_start(dst, src.rearrange("(c p) n -> p c n", p=128)).then_inc(s("const_in"), 16)
            with nc.allow_non_contiguous_dma(reason="small vectors, once"):
                act.dma_start(bq_s[:, :], bq.rearrange("(c p) -> p c", p=128)).then_inc(s("const_in"), 16)
                for dst, src, n in ((bk_s, bk, D), (bv_s, bv, D), (idx_i, sidx, U)):
                    act.dma_start(dst[:, :], src.rearrange("(a n) -> a n", a=1).to_broadcast([128, n])).then_inc(s("const_in"), 16)
            act.wait_ge(s("const_in"), 16 * CONST)
            act.wait_ge(s("pool_const"), 1)

            def exp(k, t, g):
                ge(act, f"{k}_shifted", 4 * t + g + 1, 4 * B)
                act.activation(pr[k][:, g % 2, :, :], pr[k][:, g % 2, :, :], ACT.Exp, scale=DH ** -0.5).then_inc(s(f"{k}_probs"), 1)

            def copy_T(k, t, g):
                ge(act, f"{k}_probsT", 4 * t + g + 1, 4 * B)
                ge(act, f"{k}_pv", 4 * t + g, 4 * B)
                act.activation(prT[k][:, :, :], ps_at[:, :].rearrange("p (j l) -> p j l", j=HQ), ACT.Copy)\
                    .then_inc(s(f"{k}_prT"), 1)

            def copy_o(k, t, name):
                ge(act, f"{k}_pv", 4 * t + 4, 4 * B)
                ge(act, f"{name}_oT_turned", t)
                act.activation(oT[k][:, :, :], ps_o[k][:, :].rearrange("p (g l) -> p g l", g=NQ), ACT.Copy)\
                    .then_inc(s(f"{k}_oT"), 1)

            def two(src):
                return src[:, 0:NC * L].rearrange("p (c l) -> p c l", c=NC)

            def step(u, i, par):
                if is_int(u) and u == 3:
                    act.wait_ge(s("late_in"), 16 * LATE)
                q = quads(u)
                tA, pA, tC, pC, tG = u - 1, parity(par, 1), u - 3, parity(par, 3), u - 5
                j = i - 1
                topk = par == 1 and on2(j)
                jF = (i - 3) if par else (i - 4)
                for m in range(8):
                    if m == 0 and on(tA):
                        ge(act, "a_transposed", tA + 1)
                        ge(act, "a_projected", tA)
                        act.activation(xnT[:, :, :], two(m0), ACT.Copy).then_inc(s("a_xnT"), 1)
                    if m == 1 and on(u - 6):
                        ge(act, "f_turned", u - 5)
                        ge(act, "f_gated", i - 3, B // 2)
                        act.activation(x3p[:, :, par * L:(par + 1) * L], m2[:, 256:512].rearrange("p (c l) -> p c l", c=NC),
                                       ACT.Copy).then_inc(s("f_x3T"), 1)
                    if m == 1 and par == 0 and on2(jF):
                        ge(act, "f_shifted", jF + 1)
                        act.activation(pe_[:, :, :], lg[:, :, :], ACT.Exp).then_inc(s("f_exp"), 1)
                    if m == 3 and on(tG):
                        copy_o("d", tG, "g")
                    if m == 2 and on(tC):
                        ge(act, "e_transposed", tC + 1)
                        ge(act, "e_projected", tC)
                        act.activation(cT[:, :, :], two(m2), ACT.Copy).then_inc(s("e_cT"), 1)
                    if m == 2 and on(tA):
                        ge(act, "a_projected", tA + 1)
                        ge(act, "b_scores", 4 * tA - 4, 4 * B)
                        for c in range(NC):
                            last = act.activation(qT["b"][:, pA, c, :], m0[:, c * L:(c + 1) * L], ACT.Identity,
                                                  bias=bq_s[:, c:c + 1])
                        last.then_inc(s("b_queries"), 1)
                    if m == 4 and on(tA):
                        ge(act, "a_ksbd", tA + 1)
                        ge(act, "b_keys", tA)
                        act.activation(kT[:, :, :], two(m0), ACT.Copy).then_inc(s("a_kT"), 1)
                    if m == 5 and on(tC):
                        ge(act, "c_ctx_turned", tC + 1)
                        ge(act, "c_out", tC)
                        ge(act, "a_averaged", tA + 1)
                        act.activation(ctxT[:, :, :], two(m1), ACT.Copy).then_inc(s("c_ctxT"), 1)
                    if m == 5 and on(tA):
                        ge(act, "a_averaged", tA + 1)
                        ge(act, "c_umean", tA - 1)
                        act.activation(mean_v[:, pA, :], m1[:, 256:512], ACT.Copy).then_inc(s("a_mean"), 1)
                    if m == 6 and par == 1 and on2(jF):
                        ge(act, "f_gated", jF + 1)
                        ge(act, "f_back", jF)
                        act.activation(lgT[:, :], m1[0:NE, 0:2 * L], ACT.Identity, bias=gb_s[:, 0:1]).then_inc(s("f_lgT"), 1)
                    if m == 6 and on(tC):
                        ge(act, "e_projected", tC + 1)
                        ge(act, "d_keys", tC)
                        act.activation(xkT[:, :, :], two(m2), ACT.Relu).then_inc(s("e_kT"), 1)
                        ge(act, "d_pv", 4 * tC - 4, 4 * B)
                        act.activation(vh["d"][:, pC, :, 0:DH], m2[:, 256:512].rearrange("p (h d) -> p h d", h=H),
                                       ACT.Relu).then_inc(s("d_values"), 1)
                    if m == 7 and on(tC):
                        ge(act, "c_xn_turned", tC + 1)
                        ge(act, "c_queried", tC)
                        act.activation(xn2T[:, :, :], two(m1), ACT.Copy).then_inc(s("c_xnT"), 1)
                    if m == 1 and on(tC):
                        copy_o("b", tC, "c")
                    if on(q[m - 2][1]):
                        copy_T(*q[m - 2])
                    if on(q[m][1]):
                        exp(*q[m])
                    if m == 7 and on(tC):
                        ge(act, "c_queried", tC + 1)
                        ge(act, "d_scores", 4 * tC - 4, 4 * B)
                        act.activation(qT["d"][:, pC, :, :], two(m1), ACT.Relu).then_inc(s("d_queries"), 1)
                    if m == 7 and par == 0 and on2(j):
                        ge(act, "k_turned", j + 1)
                        ge(act, "k_taken", j * 5, 5 * B)
                        act.activation(mT[0][:, :], m2[0:32, 0:L], ACT.Copy).then_inc(s("k_mT"), 1)

            run_bodies(act, step)

            def tile(i, q):
                def turned(i, q):
                    for c in range(NC):
                        ge(act, "x_turned", i * 2 + c + 1, ANY)
                        if c == 0:
                            ge(act, "h1_out", i * 2, ANY)
                        act.activation(x3T[c], bank[6 + c][:, 0:TR], ACT.Copy).then_inc(s("x_T"), 1)

                def first(i, q):
                    ge(act, "h1_out", i * 2 + 1, ANY)
                    ge(act, "h2_out", i * 2, ANY)
                    act.activation(h1[:, 0, :], bank[0][:, 0:TR], ACT.Relu, bias=wt[:, q, 3 * WL:3 * WL + 1]).then_inc(s("h1_0"), 1)

                if is_int(i) and i == 0:
                    act.wait_ge(s("tile_in0"), 48)
                    turned(0, 0)
                    first(0, 0)
                more = not is_int(i) or i + 1 < NT
                if more:
                    turned(i + 1, (q + 1) % TB)
                ge(act, "h2_out", i * 2 + 1, ANY)
                ge(act, "h3_out", i * 2, ANY)
                act.activation(h2[:, 0, :], bank[2][:, 0:TR], ACT.Relu, bias=wt[:, q, 3 * WL + NC:3 * WL + NC + 1])\
                    .then_inc(s("h2_0"), 1)
                if more:
                    first(i + 1, (q + 1) % TB)

            run_tiles(act, tile, 1)

        @block.vector
        def _(dve):
            dve.wait_ge(s("const_in"), 16 * CONST)
            dve.wait_ge(s("pool_const"), 1)
            dve.tensor_copy(idx_f[:, :], idx_i[:, :]).then_inc(s("idx"), 1)
            dve.wait_ge(s("idx"), 1)
            dve.tensor_scalar(idx_n[:, :], idx_f[:, :], 0.0, float(L), ALU.is_lt, ALU.mult).then_inc(s("idx"), 1)
            dve.wait_ge(s("idx"), 2)
            dve.tensor_tensor(idx_f[:, :], idx_f[:, :], idx_n[:, :], ALU.add).then_inc(s("idx"), 1)
            dve.wait_ge(s("idx"), 3)
            dve.tensor_scalar(idx_n[:, :], idx_f[:, :], 0.0, float(L - 1), ALU.max, ALU.min).then_inc(s("idx"), 1)
            dve.wait_ge(s("idx"), 4)
            dve.tensor_scalar(samp[:, 0:U], idx_n[:, :], kcol[:, 0:1], None, ALU.is_equal).then_inc(s("idx"), 1)
            dve.wait_ge(s("idx"), 5)
            dve.reduce_sum(smax[:, 0:1], samp[:, 0:U], AX).then_inc(s("idx"), 1)
            dve.wait_ge(s("idx"), 6)
            dve.tensor_scalar(samp[:, U:UM], smax[:, 0:1], 1.0 / U, None, ALU.mult)
            dve.tensor_copy(tri[:, :], tri_f[:, :]).then_inc(s("samp_ready"), 1)

            def quad(k, t, g, between):
                S4 = ps_s[k][:, :].rearrange("p (j l) -> p j l", j=HQ)
                ge(dve, f"{k}_scores", 4 * t + g + 1, 4 * B)
                dve.reduce_max(mx[k][:, :], S4, AX).then_inc(s(f"{k}_max"), 1)
                between()
                ge(dve, f"{k}_max", 4 * t + g + 1, 4 * B)
                ge(dve, f"{k}_probsT", 4 * t + g - 1, 4 * B)
                dve.tensor_tensor(pr[k][:, g % 2, :, :], S4, mx[k][:, :].unsqueeze(2).to_broadcast([128, HQ, L]),
                                  ALU.subtract).then_inc(s(f"{k}_shifted"), 1)

            def top_max(j, r):
                ge(dve, "k_mT", j + 1)
                ge(dve, "k_taken", j * 5 + r, ANY)
                alone(dve)
                dve.max(top8[:, :], mT[r % 2][:, :]).then_inc(s("k_max"), 1)

            def top_taken(j, r):
                ge(dve, "k_max", j * 5 + r + 1, ANY)
                alone(dve)
                dve.match_replace(mT[(r + 1) % 2][:, :], top8[:, :], mT[r % 2][:, :], GONE).then_inc(s("k_taken"), 1)

            def moments(src, stt, name):
                alone(dve)
                dve.bn_stats(stt[:, :], src).then_inc(s(f"{name}_stats"), 1)

            def gather(stt, ag, name, t):
                ge(dve, f"{name}_stats", t + 1)
                alone(dve)
                dve.bn_aggr(ag[:, :], stt[:, :]).then_inc(s(f"{name}_aggr"), 1)

            def sampled_scores(tA, pA, r, pair):
                ge(dve, "a_scored", 2 * tA + r + 1, 2 * B)
                W4 = smax[:, :].rearrange("p (c r j) -> p c r j", c=NC, r=2)
                V4 = mtok[:, pA, :].rearrange("p (c r j) -> p c r j", c=NC, r=2)
                SS = m0[:, 0:NC * HQ * UM].rearrange("p (c j u) -> p c j u", c=NC, j=HQ)
                dve.reduce_max(W4[:, :, r, :], SS[:, :, :, 0:U], AX).then_inc(s("a_smax"), 1)
                ge(dve, "a_smax", tA * 2 + r + 1, 2 * B)
                ge(dve, "k_turned", pair, B // 2)
                dve.tensor_tensor(V4[:, :, r, :], W4[:, :, r, :], SS[:, :, :, U], ALU.subtract)\
                    .then_inc(s("a_m"), 1)

            def tile(t):
                return xall[:, bass.ds(t, 1), :].rearrange("p b n -> p (b n)")

            def heads(ap):
                return ap.rearrange("p (h d) -> p h d", h=H)

            def step(u, i, par):
                if is_int(u) and u == 3:
                    dve.wait_ge(s("late_in"), 16 * LATE)
                q = quads(u)
                tA, pA, tC, pC, tG = u - 1, parity(par, 1), u - 3, parity(par, 3), u - 5
                j = i - 1
                topk = par == 1 and on2(j)
                jF = i - 4
                gate = par == 0 and on2(jF)
                for m in range(8):
                    def between():
                        if topk and m == 0:
                            top_max(j, 0)
                        if topk and m == 1:
                            top_taken(j, 1)
                        if topk and m == 2:
                            top_taken(j, 3)
                        if topk and m == 3:
                            ge(dve, "k_sel_turned", j + 1)
                            ge(dve, "c_umean", 2 * j)
                            dve.tensor_copy(sel[:, :, :], m2[:, 0:32].rearrange("p (b h) -> p b h", b=2)).then_inc(s("k_sel1"), 1)
                            dve.tensor_scalar(nsel[:, :, :], m2[:, 0:32].rearrange("p (b h) -> p b h", b=2), -1.0, 1.0,
                                              ALU.mult, ALU.add).then_inc(s("k_sel"), 1)

                    if on(q[m][1]):
                        quad(*q[m], between)
                    else:
                        between()
                    if m == 0 and gate:
                        L8 = m1[:, 0:2 * NE].rearrange("p (b e) -> p b e", b=2)
                        ge(dve, "f_back", jF + 1)
                        dve.reduce_max(gm[:, :], L8, AX).then_inc(s("f_gm"), 1)
                        ge(dve, "f_gm", jF + 1)
                        dve.tensor_tensor(lg[:, :, :], L8, gm[:, :].unsqueeze(2).to_broadcast([128, 2, NE]), ALU.subtract)\
                            .then_inc(s("f_shifted"), 1)
                    if m == 2 and gate:
                        ge(dve, "f_exp", jF + 1)
                        dve.reduce_sum(gs[:, :], pe_[:, :, :], AX).then_inc(s("f_gsum"), 1)
                        ge(dve, "f_gsum", jF + 1)
                        dve.reciprocal(gr[:, :], gs[:, :]).then_inc(s("f_grec"), 1)
                        ge(dve, "f_grec", jF + 1)
                        dve.tensor_tensor(probs[:, :, :], pe_[:, :, :], gr[:, :].unsqueeze(2).to_broadcast([128, 2, NE]),
                                          ALU.mult).then_inc(s("f_p"), 1)
                        ge(dve, "f_p", jF + 1)
                        ge(dve, "dispatched", jF * 64, ANY)
                        dve.tensor_copy(xrow[:, :, :, D + 1], probs[:, :, 0:2]).then_inc(s("f_weigh"), 1)
                        alone(dve)
                        for b in range(2):
                            last = dve.max(pt8[:, b, :], probs[:, b, :])
                        last.then_inc(s("f_top"), 1)
                    if m == 0 and topk:
                        top_taken(j, 0)
                        top_max(j, 1)
                    if m == 1 and topk and not on(tA):
                        top_max(j, 2)
                    if m == 1 and on(tA):
                        ge(dve, "a_kv", tA + 1)
                        ge(dve, "a_sampled", tA)
                        dve.tensor_tensor(ktok[:, :], m0[:, 0:D], bk_s[:, :], ALU.add).then_inc(s("a_ktok"), 1)
                        if topk:
                            top_max(j, 2)
                        ge(dve, "b_pv", 4 * tA - 4, 4 * B)
                        dve.tensor_tensor(vh["b"][:, pA, :, 0:DH], heads(m0[:, D:2 * D]), heads(bv_s[:, :]), ALU.add)\
                            .then_inc(s("b_values"), 1)
                    if m == 1 and topk:
                        top_taken(j, 2)
                        top_max(j, 3)
                    if m == 2 and topk:
                        top_max(j, 4)
                        ge(dve, "k_max", j * 5 + 5, ANY)
                        dve.tensor_copy(top2[:, 0:U % 8], top8[:, 0:U % 8]).then_inc(s("k_top2"), 1)
                        ge(dve, "k_top2", j + 1)
                        alone(dve)
                        dve.match_replace(mT[1][:, :], top2[:, :], mT[0][:, :], GONE).then_inc(s("k_taken"), 1)
                        ge(dve, "k_taken", j * 5 + 5, ANY)
                        ge(dve, "k_sel_turned", j)
                        dve.tensor_scalar(selT[:, :], mT[1][:, :], GONE, None, ALU.is_equal).then_inc(s("k_selT"), 1)
                    if m == 3 and on(tC):
                        jC = (i - 1) if par else (i - 2)
                        O = m1[:, :].rearrange("p (h e) -> p h e", h=H)
                        ge(dve, "c_oT_turned", tC + 1)
                        dve.reciprocal(rden[:, :], O[:, :, DH]).then_inc(s("c_rden"), 1)
                        ge(dve, "c_rden", tC + 1)
                        ge(dve, "k_sel", jC + 1)
                        dve.tensor_tensor(wsel[:, :], rden[:, :], sel[:, pC, :], ALU.mult).then_inc(s("c_wsel"), 1)
                        ge(dve, "c_wsel", tC + 1)
                        dve.tensor_tensor(heads(ctxa[:, :]), O[:, :, 0:DH],
                                          wsel[:, :].unsqueeze(2).to_broadcast([128, H, DH]), ALU.mult)\
                            .then_inc(s("c_scaled"), 1)
                        ge(dve, "c_scaled", tC + 1)
                        ge(dve, "c_umean", tC + 1)
                        ge(dve, "c_ctx_turned", tC)
                        dve.tensor_tensor(ctxv[:, :], ctxa[:, :], umean[:, :], ALU.add).then_inc(s("c_context"), 1)
                    if m == 3 and gate:
                        ge(dve, "f_top", jF + 1)
                        alone(dve)
                        for b in range(2):
                            last = dve.max_index(pi8[:, b, :], pt8[:, b, :], probs[:, b, :])
                        last.then_inc(s("f_ti"), 1)
                        ge(dve, "f_ti", jF + 1)
                        dve.tensor_copy(pf2[:, :, :], pi8[:, :, 0:2]).then_inc(s("f_tf"), 1)
                        ge(dve, "f_tf", jF + 1)
                        dve.tensor_tensor(oh[:, :, :, :].rearrange("p b k e -> p (b k) e"),
                                          iota8[:, :].unsqueeze(1).to_broadcast([128, 4, NE]),
                                          pf2[:, :, :].rearrange("p b k -> p (b k)").unsqueeze(2).to_broadcast([128, 4, NE]),
                                          ALU.is_equal).then_inc(s("f_oh"), 1)
                        ge(dve, "f_oh", jF + 1)
                        ge(dve, "f_chosen", jF)
                        dve.tensor_tensor(both[:, :, :], oh[:, :, 0, :], oh[:, :, 1, :], ALU.add).then_inc(s("f_both"), 1)
                    if m == 3 and on(tA):
                        ge(dve, "a_sampled", tA + 1)
                        ge(dve, "a_scored", 2 * tA, 2 * B)
                        dve.tensor_tensor(ksbd[:, :, :, :],
                                          m0[:, 256:256 + NC * UM].rearrange("p (c u) -> p c u", c=NC).unsqueeze(2)
                                          .to_broadcast([128, NC, HQ, UM]),
                                          hmask[:, :].unsqueeze(1).unsqueeze(3).to_broadcast([128, NC, HQ, UM]),
                                          ALU.mult).then_inc(s("a_ksbd"), 1)
                    if m == 4 and on(tG):
                        O = m2[:, :].rearrange("p (h e) -> p h e", h=H)
                        ge(dve, "g_oT_turned", tG + 1)
                        dve.reciprocal(xrden[:, :], O[:, :, DH]).then_inc(s("g_rden"), 1)
                        ge(dve, "g_rden", tG + 1)
                        dve.tensor_tensor(heads(xatt[:, :]), O[:, :, 0:DH],
                                          xrden[:, :].unsqueeze(2).to_broadcast([128, H, DH]), ALU.mult)\
                            .then_inc(s("g_scaled"), 1)
                        ge(dve, "g_scaled", tG + 1)
                        dve.tensor_tensor(tile(tG), xatt[:, :], tile(tG), ALU.add).then_inc(s("g_x2"), 1)
                    if m == 4 and on(tG):
                        ge(dve, "g_x2", tG + 1)
                        ge(dve, "f_norm", tG)
                        ge(dve, "f_veps", tG)
                        moments(tile(tG), stf, "f")
                        gather(stf, agf, "f", tG)
                    if m == 5 and on(tA):
                        sampled_scores(tA, pA, 0, i if par else i - 1)
                    if m == 5 and on(tC):
                        ge(dve, "c_out", tC + 1)
                        ge(dve, "c_xb", tC + 1)
                        dve.tensor_tensor(tile(tC), m1[:, 0:D], tile(tC), ALU.add).then_inc(s("c_x1"), 1)
                    if m == 5 and on(u):
                        ge(dve, f"x_in{par}", i * 16 + 16, 16 * B)
                        ge(dve, "l_rstd", u)
                        moments(tile(u), stl, "l")
                    if m == 5 and on(tC):
                        ge(dve, "c_x1", tC + 1)
                        moments(tile(tC), stc, "c")
                    if m == 5 and on(u):
                        gather(stl, agl, "l", u)
                    if m == 5 and on(tC):
                        gather(stc, agc, "c", tC)
                    if m == 6 and gate:
                        ge(dve, "f_pos", jF + 1)
                        dve.tensor_tensor(posE[:, :, :], m1[:, 0:2 * NE].rearrange("p (b e) -> p b e", b=2),
                                          row0[:, :].unsqueeze(1).to_broadcast([128, 2, NE]), ALU.add).then_inc(s("f_posE"), 1)
                    if m == 6 and on(tC):
                        ge(dve, "c_rstd", tC + 1)
                        ge(dve, "c_aggr", tC + 1)
                        ge(dve, "c_xn_turned", tC)
                        dve.tensor_scalar(xn2[:, :], tile(tC), agc[:, 0:1], rsc[:, 1:2], ALU.subtract, ALU.mult)\
                            .then_inc(s("c_xn"), 1)
                    if m == 6 and on(u):
                        ge(dve, "l_rstd", u + 1)
                        ge(dve, "l_aggr", u + 1)
                        ge(dve, "a_transposed", u - 1)
                        dve.tensor_scalar(xn[:, par, :], tile(u), agl[:, 0:1], rsl[:, 1:2], ALU.subtract, ALU.mult)\
                            .then_inc(s("l_xn"), 1)
                    if m == 6 and on(tA):
                        sampled_scores(tA, pA, 1, i if par else i - 1)
                    if m == 6 and gate:
                        ge(dve, "f_posE", jF + 1)
                        for b in range(2):
                            last = dve.tensor_tensor(ohp[:, b, :, :], oh[:, b, :, :],
                                                     posE[:, b:b + 1, :].to_broadcast([128, 2, NE]), ALU.mult)
                        last.then_inc(s("f_ohp"), 1)
                        ge(dve, "f_ohp", jF + 1)
                        dve.reduce_sum(slot_f[:, :, :].rearrange("p b k -> p (b k)"),
                                       ohp[:, :, :, :].rearrange("p b k e -> p (b k) e"), AX).then_inc(s("f_slotf"), 1)
                        ge(dve, "f_slotf", jF + 1)
                        dve.tensor_copy(slot[:, :, :], slot_f[:, :, :]).then_inc(s("f_slot"), 1)
                    if m == 7 and on(tG):
                        ge(dve, "f_norm", tG + 1)
                        ge(dve, "f_rstd", tG + 1)
                        ge(dve, "f_turned", tG - 1)
                        dve.tensor_scalar(xn3[:, parity(par, 5), :], tile(tG), norm3[:, bass.ds(tG, 1), 0],
                                          norm3[:, bass.ds(tG, 1), 1], ALU.subtract, ALU.mult).then_inc(s("f_xn"), 1)
                    if m == 7 and gate:
                        ge(dve, "f_norm", jF * 2 + 2)
                        ge(dve, "f_rstd", jF * 2 + 2)
                        for b in range(2):
                            for k in range(2):
                                dve.tensor_scalar(xrow[:, b, k, 0:D], tile(jF * 2 + b),
                                                  norm3[:, bass.ds(jF * 2 + b, 1), 0], norm3[:, bass.ds(jF * 2 + b, 1), 1],
                                                  ALU.subtract, ALU.mult)
                        dve.tensor_copy(xrow[:, :, :, D], token[:, bass.ds(jF * 2, 2)].unsqueeze(2).to_broadcast([128, 2, 2]))\
                            .then_inc(s("f_rows"), 1)

            run_bodies(dve, step)

            def link(ins):
                links[0] += 1
                ins.then_inc(s("t_link"), 1)
                dve.wait_ge(s("t_link"), links[0])

            links = [0]
            dve.wait_ge(s("t_counted"), 1)
            link(dve.tensor_tensor(pad0[:, :], m1[:, 0:NE], row0[:, :], ALU.add))
            link(dve.tensor_copy(cnt[:, :], m1[:, 0:NE]))
            dve.tensor_copy(pad_i[:, :], pad0[:, :]).then_inc(s("t_pads"), 1)
            link(dve.tensor_tensor(cmpS[:, :, :], cnt[:, :].unsqueeze(2).to_broadcast([128, NE, SL]),
                                   steps_c[:, :].unsqueeze(1).to_broadcast([128, NE, SL]), ALU.is_gt))
            link(dve.reduce_sum(nt[:, :], cmpS[:, :, :], AX))
            link(dve.tensor_tensor(ntm[:, :, :], upto[:, :, :], nt[:, :].unsqueeze(1).to_broadcast([128, NE, NE]), ALU.mult))
            link(dve.reduce_sum(cum[:, :], ntm[:, :, :], AX))
            link(dve.tensor_tensor(cmpT[:, :, :], tile_c[:, :].unsqueeze(2).to_broadcast([128, NT, NE]),
                                   cum[:, :].unsqueeze(1).to_broadcast([128, NT, NE]), ALU.is_ge))
            link(dve.reduce_sum(te[:, :], cmpT[:, :, :], AX))
            link(dve.tensor_tensor(cmpN[:, :, :], cmpT[:, :, :], nt[:, :].unsqueeze(1).to_broadcast([128, NT, NE]), ALU.mult))
            link(dve.reduce_sum(tn[:, :], cmpN[:, :, :], AX))
            link(dve.tensor_tensor(tn[:, :], tile_c[:, :], tn[:, :], ALU.subtract))
            link(dve.tensor_scalar(tn[:, :], tn[:, :], float(TR), None, ALU.mult))
            link(dve.tensor_scalar(trow[:, :], te[:, :], float(RC), None, ALU.mult))
            link(dve.tensor_tensor(trow[:, :], trow[:, :], tn[:, :], ALU.add))
            link(dve.tensor_scalar(trow[:, :], trow[:, :], float(NE * RC), None, ALU.min))
            link(dve.tensor_scalar(te[:, :], te[:, :], float(NE - 1), None, ALU.min))
            link(dve.tensor_copy(te_i[:, :], te[:, :]))
            dve.tensor_copy(trow_i[:, :], trow[:, :]).then_inc(s("t_table"), 1)

            def tile_of_expert(i, q):
                def first(i, q):
                    dve.wait_ge(s(f"tile_in{q}"), tiles_in(i, q))
                    ge(dve, "y_out", (i - TB + 1) * (16 * TS), ANY)
                    dve.tensor_copy(dest[:, q, :], xs[:, q, :, D]).then_inc(s("x_dest"), 1)
                    ge(dve, "h1_out", i * 2 + 2, ANY)
                    ge(dve, "h2_out", i * 2, ANY)
                    dve.tensor_scalar(h1[:, 1, :], bank[1][:, 0:TR], wt[:, q, 3 * WL + 1:3 * WL + 2], 0.0, ALU.add, ALU.max)\
                        .then_inc(s("h1_1"), 1)

                if is_int(i) and i == 0:
                    first(0, 0)
                ge(dve, "h2_out", i * 2 + 2, ANY)
                ge(dve, "h3_out", i * 2, ANY)
                dve.tensor_scalar(h2[:, 1, :], bank[3][:, 0:TR], wt[:, q, 3 * WL + NC + 1:3 * WL + NC + 2], 0.0, ALU.add, ALU.max)\
                    .then_inc(s("h2_1"), 1)
                if not is_int(i) or i + 1 < NT:
                    first(i + 1, (q + 1) % TB)
                for hf, subs in enumerate(HALVES):
                    n = len(subs)
                    ge(dve, "h3_out", i * 2 + hf + 1, ANY)
                    ge(dve, "y_out", (i - TB + 1) * (16 * TS), ANY)
                    dve.tensor_tensor(y[:, q, subs[0]:subs[0] + n, :],
                                      bank[4 + hf][:, 0:n * D].rearrange("p (t n) -> p t n", t=n),
                                      b3r[:, q:q + 1, :].to_broadcast([128, n, D]), ALU.add).then_inc(s("y_sum"), 1)
                for hf, subs in enumerate(HALVES):
                    ge(dve, "y_sum", i * 2 + hf + 1, ANY)
                    for sub in subs:
                        dve.tensor_scalar(y[:, q, sub, :], y[:, q, sub, :], xs[:, q, sub, D + 1:D + 2], None, ALU.mult)\
                            .then_inc(s("y_ready"), 1)

            run_tiles(dve, tile_of_expert, 1)

        @block.tensor
        def _(pe):
            mm = nc.tensor.matmul

            def scores(k, t, g, p):
                c, r = g // 2, g % 2
                rows = slice(64 * r, 64 * r + 64)
                if g == 0:
                    ge(pe, f"{k}_queries", t + 1)
                    ge(pe, f"{k}_keys", t + 1)
                ge(pe, f"{k}_shifted", 4 * t + g, 4 * B)
                mm(ps_s[k][:, :], qT[k][rows, p, c, :], kbd[k][rows, p, c, :, :].rearrange("p j l -> p (j l)"),
                   start=True, stop=True).then_inc(s(f"{k}_scores"), 1)

            def turn_probs(k, t, g):
                ge(pe, f"{k}_probs", 4 * t + g + 1, 4 * B)
                if k == "b":
                    ge(pe, "d_prT", 4 * (t - 2) + g, 4 * B)
                    if is_int(t):
                        ge(pe, "b_prT", 4 * t + g, 4 * B)
                else:
                    ge(pe, "b_prT", 4 * (t + 2) + g + 1, 4 * B)
                    if is_int(t):
                        ge(pe, "d_prT", 4 * t + g, 4 * B)
                for j in range(HQ):
                    last = nc.tensor.transpose(ps_at[:, j * L:(j + 1) * L], pr[k][:, g % 2, j, :], ident[:, :])
                last.then_inc(s(f"{k}_probsT"), 1)

            def pv(k, t, g, p):
                ge(pe, f"{k}_prT", 4 * t + g + 1, 4 * B)
                if g == 0:
                    ge(pe, f"{k}_values", t + 1)
                    ge(pe, f"{k}_oT", t)
                for j in range(HQ):
                    last = mm(ps_o[k][HS * j:HS * j + HS, g * L:(g + 1) * L], vh[k][:, p, HQ * g + j, :], prT[k][:, j, :],
                              start=True, stop=True, skip_group_check=True)
                last.then_inc(s(f"{k}_pv"), 1)

            def turn(dst, src, n=NC):
                for c in range(n):
                    last = nc.tensor.transpose(dst[:, c * L:(c + 1) * L], src[:, c * 128:(c + 1) * 128], ident[:, :])
                return last

            def rows_out(dst, w, src):
                for c in range(NC):
                    for k in range(NC):
                        last = mm(dst[:, c * L:(c + 1) * L], w[:, k, c * 128:(c + 1) * 128], src[:, k, :],
                                  start=(k == 0), stop=(k == NC - 1))
                return last

            pe.wait_ge(s("const_in"), 16 * CONST)
            pe.wait_ge(s("pool_const"), 1)
            pe.wait_ge(s("samp_ready"), 1)

            def step(u, i, par):
                if is_int(u) and u == 3:
                    pe.wait_ge(s("late_in"), 16 * LATE)
                q = quads(u)
                tA, pA, tC, pC, tG = u - 1, parity(par, 1), u - 3, parity(par, 3), u - 5
                j = i - 1
                topk = par == 1 and on2(j)
                for m in range(8):
                    k, t, g = q[m]
                    if on(t):
                        scores(k, t, g, par)
                    if m == 0 and on(tA):
                        ge(pe, "l_xn", tA + 1)
                        ge(pe, "a_m", 2 * tA, 2 * B)
                        turn(m0, xn[:, pA, :]).then_inc(s("a_transposed"), 1)
                    if m == 0 and par == 0 and on2(i - 4):
                        ge(pe, "f_lgT", i - 4 + 1)
                        ge(pe, "d_queries", u - 3)
                        alone(pe)
                        for b in range(2):
                            last = nc.tensor.transpose(m1[:, b * NE:(b + 1) * NE], lgT[:, b * L:(b + 1) * L], ident[0:NE, 0:NE])
                        last.then_inc(s("f_back"), 1)
                    if m == 1 and on(tA):
                        ge(pe, "a_xnT", tA + 1)
                        for k in range(NC):
                            last = mm(m0[:, :], xnT[:, k, :], wkv_s[:, k, :], start=(k == 0), stop=(k == NC - 1))
                        last.then_inc(s("a_kv"), 1)
                    if m == 1 and on(q[-2][1]):
                        pv(*q[-2], 1 - par)
                    if m == 2 and on(tC):
                        ge(pe, "b_oT", tC + 1)
                        ge(pe, "d_queries", tC)
                        if par == 0 and on2(i - 4):
                            ge(pe, "f_shifted", i - 4 + 1)
                        turn(m1, oT["b"][:, :, :].rearrange("p g l -> p (g l)"), NQ).then_inc(s("c_oT_turned"), 1)
                    if m == 2 and on(tA):
                        ge(pe, "a_ktok", tA + 1)
                        ge(pe, "b_values", tA + 1)
                        rows_out(m0, wq_s, xnT).then_inc(s("a_projected"), 1)
                    if m == 3 and topk:
                        ge(pe, "k_selT", j + 1)
                        ge(pe, "e_cT", tC + 1)
                        alone(pe)
                        nc.tensor.transpose(m2[:, 0:32], selT[:, :], ident[0:32, 0:32]).then_inc(s("k_sel_turned"), 1)
                    if m == 3 and on(tA):
                        ge(pe, "b_queries", tA + 1)
                        turn(m0, ktok)
                        for c in range(NC):
                            last = mm(m0[:, 256 + c * UM:256 + (c + 1) * UM], ktok[:, c * 128:(c + 1) * 128], samp[:, :],
                                      start=True, stop=True)
                        last.then_inc(s("a_sampled"), 1)
                    if m == 4 and on(tG):
                        ge(pe, "d_oT", tG + 1)
                        ge(pe, "e_cT", tC + 1)
                        if topk:
                            ge(pe, "k_sel", j + 1)
                        turn(m2, oT["d"][:, :, :].rearrange("p g l -> p (g l)"), NQ).then_inc(s("g_oT_turned"), 1)
                    if m == 6 and on(tC):
                        ge(pe, "g_scaled", tG + 1)
                        ge(pe, "e_cT", tC + 1)
                        if topk:
                            ge(pe, "k_sel", j + 1)
                        rows_out(m2, xwk_s, cT)
                        for k in range(NC):
                            last = mm(m2[:, 256:512], cT[:, k, :], xwv_s[:, k, :], start=(k == 0), stop=(k == NC - 1))
                        last.then_inc(s("e_projected"), 1)
                    if m in (5, 6) and on(tA):
                        r = m - 5
                        if r == 0:
                            ge(pe, "a_kT", tA + 1)
                            ge(pe, "a_ksbd", tA + 1)
                        else:
                            ge(pe, "a_m", 2 * tA + 1, 2 * B)
                        rows = slice(64 * r, 64 * r + 64)
                        for c in range(NC):
                            last = mm(m0[:, c * HQ * UM:(c + 1) * HQ * UM], qT["b"][rows, pA, c, :],
                                      ksbd[rows, c, :, :].rearrange("p j u -> p (j u)"), start=True, stop=True)
                        last.then_inc(s("a_scored"), 1)
                    if m == 6 and par == 1 and on2(i - 3):
                        ge(pe, "f_x3T", i * 2 - 4)
                        ge(pe, "c_x1", tC + 1)
                        for k in range(NC):
                            last = mm(m1[0:NE, 0:2 * L], gw_s[:, k, :], x3p[:, k, :], start=(k == 0), stop=(k == NC - 1))
                        last.then_inc(s("f_gated"), 1)
                    if m == 6 and par == 0 and on2(i - 4):
                        ge(pe, "f_both", i - 4 + 1)
                        ge(pe, "f_before", i - 4 + 1)
                        ge(pe, "f_before0", i - 4 + 1)
                        ge(pe, "c_x1", tC + 1)
                        P8 = m1[:, 0:2 * NE]
                        mm(P8, ones[:, :], before[:, :, :].rearrange("p b e -> p (b e)"), start=True, stop=False)
                        mm(P8, tri[:, :], both[:, :, :].rearrange("p b e -> p (b e)"), start=False, stop=True)\
                            .then_inc(s("f_pos"), 1)
                    if m == 7 and on(tC):
                        ge(pe, "c_xn", tC + 1)
                        if par == 1 and on2(i - 3):
                            ge(pe, "f_lgT", i - 3 + 1)
                        if par == 0 and on2(i - 4):
                            ge(pe, "f_posE", i - 4 + 1)
                        turn(m1, xn2).then_inc(s("c_xn_turned"), 1)
                    if on(q[m - 3][1]) and m != 1:
                        pv(*q[m - 3], par if m >= 3 else 1 - par)
                    if on(q[m - 2][1]):
                        turn_probs(*q[m - 2])
                    if m == 0 and on(u - 6):
                        ge(pe, "f_xn", u - 5)
                        ge(pe, "e_kT", tC)
                        ge(pe, "d_values", tC)
                        ge(pe, "g_scaled", tG)
                        if topk:
                            ge(pe, "k_mT", j + 1)
                        turn(m2[:, 256:512], xn3[:, par, :]).then_inc(s("f_turned"), 1)
                    if m == 1 and on(tC):
                        jC = (i - 1) if par else (i - 2)
                        ge(pe, f"ctx_in{pC}", jC * 16 + 16, 16 * B)
                        ge(pe, "e_kT", tC)
                        ge(pe, "d_values", tC)
                        ge(pe, "f_x3T", u - 5)
                        if topk:
                            ge(pe, "k_mT", j + 1)
                        turn(m2, cin[:, pC, :]).then_inc(s("e_transposed"), 1)
                    if m == 4 and on(tC):
                        ge(pe, "c_context", tC + 1)
                        turn(m1, ctxv).then_inc(s("c_ctx_turned"), 1)
                    if m == 4 and on(tA):
                        ge(pe, "a_mean", tA)
                        ge(pe, "b_values", tA + 1)
                        mm(m1[:, 256:512].rearrange("p (h d) -> p h d", h=H), mean_w[:, :], vh["b"][:, pA, :, 0:DH],
                           start=True, stop=True).then_inc(s("a_averaged"), 1)
                    if m == 5 and on(tC):
                        ge(pe, "c_ctxT", tC + 1)
                        ge(pe, "a_mean", tA + 1)
                        for k in range(NC):
                            last = mm(m1[:, 0:D], ctxT[:, k, :], wo_s[:, k, :], start=(k == 0), stop=(k == NC - 1))
                        last.then_inc(s("c_out"), 1)
                    if m == 7 and on(tC):
                        ge(pe, "c_xnT", tC + 1)
                        rows_out(m1, xwq_s, xn2T).then_inc(s("c_queried"), 1)
                    if m == 7 and par == 0 and on2(j):
                        ge(pe, "a_m", j * 4 + 4, 2 * B)
                        ge(pe, "e_kT", tC + 1)
                        ge(pe, "d_values", tC + 1)
                        ge(pe, "g_scaled", tG + 1)
                        nc.tensor.transpose(m2[0:32, 0:L], mtok[:, :, :].rearrange("p b h -> p (b h)"), ident[:, :])\
                            .then_inc(s("k_turned"), 1)

            run_bodies(pe, step)

            pe.wait_ge(s("f_chosen"), B // 2)
            pe.wait_ge(s("f_posE"), B // 2)
            pe.wait_ge(s("d_queries"), B)
            mm(m1[:, 0:NE], ones[:, :], chosen[:, :], start=True, stop=True).then_inc(s("t_counted"), 1)

            def weights(q, layer):
                return wt[:, q, layer * WL:(layer + 1) * WL].rearrange("p (k n) -> p k n", k=NC)

            def turn_rows(i, q):
                pe.wait_ge(s(f"tile_in{q}"), tiles_in(i, q))
                for c in range(NC):
                    ge(pe, "x_T", i * 2 + c - 1, ANY)
                    for sub in range(TS):
                        last = nc.tensor.transpose(bank[6 + c][:, sub * 128:(sub + 1) * 128],
                                                   xs[:, q, sub, c * 128:(c + 1) * 128], ident[:, :])
                    last.then_inc(s("x_turned"), 1)

            def layer1(i, q):
                ge(pe, "x_T", i * 2 + 2, ANY)
                for c in range(NC):
                    ge(pe, f"h1_{c}", i, ANY)
                    for k in range(NC):
                        last = mm(bank[c][:, 0:TR], weights(q, 0)[:, k, c * 128:(c + 1) * 128], x3T[k],
                                  start=(k == 0), stop=(k == NC - 1))
                    last.then_inc(s("h1_out"), 1)

            def tile(i, q):
                if is_int(i) and i == 0:
                    turn_rows(0, 0)
                    layer1(0, 0)
                more = not is_int(i) or i + 1 < NT
                if more:
                    turn_rows(i + 1, (q + 1) % TB)
                ge(pe, "h1_0", i + 1, ANY)
                ge(pe, "h1_1", i + 1, ANY)
                for c in range(NC):
                    ge(pe, f"h2_{c}", i, ANY)
                    for k in range(NC):
                        last = mm(bank[2 + c][:, 0:TR], weights(q, 1)[:, k, c * 128:(c + 1) * 128], h1[:, k, :],
                                  start=(k == 0), stop=(k == NC - 1))
                    last.then_inc(s("h2_out"), 1)
                if more:
                    layer1(i + 1, (q + 1) % TB)
                ge(pe, "h2_0", i + 1, ANY)
                ge(pe, "h2_1", i + 1, ANY)
                for hf, subs in enumerate(HALVES):
                    ge(pe, "y_sum", i * 2 + hf - 1, ANY)
                    for t, sub in enumerate(subs):
                        for k in range(NC):
                            rows = slice(sub * 128, (sub + 1) * 128)
                            last = mm(bank[4 + hf][:, t * D:(t + 1) * D], h2[:, k, rows], weights(q, 2)[:, k, :],
                                      start=(k == 0), stop=(k == NC - 1))
                    last.then_inc(s("h3_out"), 1)

            run_tiles(pe, tile, 1)


_OUT = ((B, L, D), "float32")


def kernel(**inputs):
    import numpy as np
    import concourse.bacc as bacc
    from concourse import mybir as mb
    from concourse.bass_utils import run_bass_kernel_spmd

    a = {k: np.ascontiguousarray(v) for k, v in inputs.items()}
    p = "L0_attn_"
    f = "L0_ffn_"
    data = {"x": a["x"], "ctx": a["ctx_1024"], "wq": a[p + "W_q"], "bq": a[p + "b_q"], "wk": a[p + "W_k"],
            "bk": a[p + "b_k"], "wv": a[p + "W_v"], "bv": a[p + "b_v"], "wo": a[p + "W_o"], "bo": a[p + "b_o"],
            "sidx": a[p + "k_sample_idx"],
            "xwqT": np.ascontiguousarray(a["L0_xattn_Wq"].T), "xwkT": np.ascontiguousarray(a["L0_xattn_Wk"].T),
            "xwvT": np.ascontiguousarray(a["L0_xattn_Wv"].T),
            "gwT": np.ascontiguousarray(a[f + "gate_w"].T), "gb": a[f + "gate_b"],
            "experts": np.concatenate(
                [a[f + w].reshape(NE, NC, 128, D).transpose(0, 2, 1, 3).reshape(NE, 128, WL) for w in ("w1", "w2", "w3")]
                + [a[f + b].reshape(NE, NC, 128).transpose(0, 2, 1) for b in ("b1", "b2")], axis=2),
            "b3": a[f + "b3"],
            "ident_d": np.eye(128, dtype=np.float32),
            "hmask_d": (np.arange(128)[:, None] % 64 // 16 == np.arange(4)[None, :]).astype(np.float32),
            "iota8_d": np.tile(np.arange(8, dtype=np.float32), (128, 1)),
            "kcol_d": np.arange(128, dtype=np.float32)[:, None],
            "tri_d": np.triu(np.ones((128, 128), np.float32), 1),
            "token_d": (np.arange(128)[:, None] + 128 * np.arange(B)[None, :]).astype(np.float32),
            "row0_d": np.tile(RC * np.arange(NE, dtype=np.float32), (128, 1)),
            "steps_d": np.tile(TR * np.arange(SL, dtype=np.float32), (128, 1)),
            "upto_d": np.tile(np.tril(np.ones((NE, NE), np.float32)), (128, 1, 1)),
            "tiles_d": np.tile(np.arange(NT, dtype=np.float32), (128, 1))}
    nc = bacc.Bacc("TRN2", target_bir_lowering=False, num_devices=1)
    arrays, args = {}, []
    for name, v in data.items():
        arrays[f"in_{name}"] = v
        args.append(nc.dram_tensor(f"in_{name}", v.shape, mb.dt.from_np(v.dtype), kind="ExternalInput").ap())
    args.append(nc.dram_tensor("out_0", _OUT[0], mb.dt.float32, kind="ExternalOutput").ap())
    decoder_block(nc, *args)
    r = run_bass_kernel_spmd(nc, [arrays], core_ids=[0])
    return r.results[0]["out_0"]
```
